# Optimizing a Trainium2 kernel written in Bass

```python
import numpy as np
import jax
import jax.numpy as jnp

def _softmax(x, axis=-1):
    return jax.nn.softmax(x, axis=axis)

def _gelu(x):
    return jax.nn.gelu(x, approximate=True)

def _silu(x):
    return jax.nn.silu(x)

def _sigmoid(x):
    return jax.nn.sigmoid(x)

def _layernorm(x, axis=-1, eps=1e-05):
    m = jnp.mean(x, axis=axis, keepdims=True)
    v = jnp.var(x, axis=axis, keepdims=True)
    return (x - m) / jnp.sqrt(v + eps)

def _scatter_add(tgt, idx, src, axis=0):
    return tgt.at[idx].add(src)

def _segment_sum(src, seg, n):
    return jax.ops.segment_sum(src, seg, n)
kernel_name = 'mk_macaron_d2_jaxref_r8_51d94d'

def setup_inputs(seed: int=0):
    np.random.seed(seed)
    _w = jnp.asarray

    def _L0_attn_setup():
        import jax, jax.numpy as jnp
        import numpy as np
        B, S, H, NH = (1, 512, 128, 16)
        DH = H // NH

        def _split_heads(x):
            b, s, h = x.shape
            return jnp.transpose(x.reshape(b, s, NH, DH), (0, 2, 1, 3))
        key = jax.random.key(seed)
        ks = jax.random.split(key, 9)
        sc = 0.02
        return {'queries': jax.random.normal(ks[0], (B, S, H), jnp.float32), 'keys': jax.random.normal(ks[1], (B, S, H), jnp.float32), 'values': jax.random.normal(ks[2], (B, S, H), jnp.float32), 'Wq_w': jax.random.normal(ks[3], (H, H), jnp.float32) * sc, 'Wq_b': jax.random.normal(ks[4], (H,), jnp.float32) * sc, 'Wk_w': jax.random.normal(ks[5], (H, H), jnp.float32) * sc, 'Wk_b': jax.random.normal(ks[6], (H,), jnp.float32) * sc, 'Wv_w': jax.random.normal(ks[7], (H, H), jnp.float32) * sc, 'Wv_b': jax.random.normal(ks[8], (H,), jnp.float32) * sc}
    _L0_attn_in = _L0_attn_setup()

    def _L0_ffn_setup():
        import jax, jax.numpy as jnp
        import numpy as np
        TOPK = 2
        CAPACITY_FACTOR = 1.0
        EPS = 1e-06
        B, S, D = (4, 512, 128)
        E = 8
        SUB_H = 256 // E
        key = jax.random.key(seed)
        ks = jax.random.split(key, 7)
        x = jax.random.normal(ks[0], (B, S, D), dtype=jnp.float32)
        w_gate_w = jax.random.normal(ks[1], (D, E), dtype=jnp.float32) * 0.02
        w_gate_b = jnp.zeros((E,), jnp.float32)
        W1 = jax.random.normal(ks[2], (E, D, SUB_H), dtype=jnp.float32) * 0.02
        b1 = jnp.zeros((E, SUB_H), jnp.float32)
        W2 = jax.random.normal(ks[3], (E, SUB_H, D), dtype=jnp.float32) * 0.02
        b2 = jnp.zeros((E, D), jnp.float32)
        return {'x': x, 'w_gate_w': w_gate_w, 'w_gate_b': w_gate_b, 'W1': W1, 'b1': b1, 'W2': W2, 'b2': b2}
    _L0_ffn_in = _L0_ffn_setup()

    def _L1_attn_setup():
        import jax, jax.numpy as jnp
        import numpy as np
        D_MODEL = 128
        N_HEADS = 16
        LN_EPS = 1e-06

        def _layernorm(t, scale):
            mu = jnp.mean(t, axis=-1, keepdims=True)
            var = jnp.var(t, axis=-1, keepdims=True)
            return (t - mu) * jax.lax.rsqrt(var + LN_EPS) * scale
        key = jax.random.key(seed)
        k1, k2, k3 = jax.random.split(key, 3)
        B, S = (2, 256)
        x = jax.random.normal(k1, (B, S, D_MODEL), dtype=jnp.float32)
        W_qkv = jax.random.normal(k2, (D_MODEL, 3 * D_MODEL), dtype=jnp.float32) / np.sqrt(D_MODEL)
        W_out = jax.random.normal(k3, (D_MODEL, D_MODEL), dtype=jnp.float32) / np.sqrt(D_MODEL)
        q_scale = jnp.ones((D_MODEL,), dtype=jnp.float32)
        k_scale = jnp.ones((D_MODEL,), dtype=jnp.float32)
        return {'x': x, 'W_qkv': W_qkv, 'q_scale': q_scale, 'k_scale': k_scale, 'W_out': W_out}
    _L1_attn_in = _L1_attn_setup()

    def _L1_ffn_setup():
        import jax, jax.numpy as jnp
        import numpy as np
        B, S, D = (4, 256, 128)
        O = 128
        E = 8
        K = 2
        key = jax.random.key(seed)
        k1, k2, k3, k4, k5 = jax.random.split(key, 5)
        scale = 1.0 / np.sqrt(D)
        x = jax.random.normal(k1, (B, S, D), dtype=jnp.float32)
        We = jax.random.uniform(k2, (E, D, O), dtype=jnp.float32, minval=-scale, maxval=scale)
        be = jax.random.uniform(k3, (E, O), dtype=jnp.float32, minval=-scale, maxval=scale)
        Wg = jax.random.uniform(k4, (D, E), dtype=jnp.float32, minval=-scale, maxval=scale)
        bg = jax.random.uniform(k5, (E,), dtype=jnp.float32, minval=-scale, maxval=scale)
        return {'x': x, 'We': We, 'be': be, 'Wg': Wg, 'bg': bg}
    _L1_ffn_in = _L1_ffn_setup()
    _d = {'L0_attn_queries': _L0_attn_in['queries'], 'L0_attn_keys': _L0_attn_in['keys'], 'L0_attn_values': _L0_attn_in['values'], 'L0_attn_Wq_w': _L0_attn_in['Wq_w'], 'L0_attn_Wq_b': _L0_attn_in['Wq_b'], 'L0_attn_Wk_w': _L0_attn_in['Wk_w'], 'L0_attn_Wk_b': _L0_attn_in['Wk_b'], 'L0_attn_Wv_w': _L0_attn_in['Wv_w'], 'L0_attn_Wv_b': _L0_attn_in['Wv_b'], 'L0_ffn_w_gate_w': _L0_ffn_in['w_gate_w'], 'L0_ffn_w_gate_b': _L0_ffn_in['w_gate_b'], 'L0_ffn_W1': _L0_ffn_in['W1'], 'L0_ffn_b1': _L0_ffn_in['b1'], 'L0_ffn_W2': _L0_ffn_in['W2'], 'L0_ffn_b2': _L0_ffn_in['b2'], 'L1_attn_W_qkv': _L1_attn_in['W_qkv'], 'L1_attn_q_scale': _L1_attn_in['q_scale'], 'L1_attn_k_scale': _L1_attn_in['k_scale'], 'L1_attn_W_out': _L1_attn_in['W_out'], 'L1_ffn_We': _L1_ffn_in['We'], 'L1_ffn_be': _L1_ffn_in['be'], 'L1_ffn_Wg': _L1_ffn_in['Wg'], 'L1_ffn_bg': _L1_ffn_in['bg']}
    _x0 = _d['L0_attn_queries']
    _d['L0_attn_queries'] = jax.random.normal(jax.random.fold_in(jax.random.key(seed), 1), (2, 1024, 128), dtype=_x0.dtype)
    del _x0
    return _d

def reference(L0_attn_queries, L0_attn_keys, L0_attn_values, L0_attn_Wq_w, L0_attn_Wq_b, L0_attn_Wk_w, L0_attn_Wk_b, L0_attn_Wv_w, L0_attn_Wv_b, L0_ffn_w_gate_w, L0_ffn_w_gate_b, L0_ffn_W1, L0_ffn_b1, L0_ffn_W2, L0_ffn_b2, L1_attn_W_qkv, L1_attn_q_scale, L1_attn_k_scale, L1_attn_W_out, L1_ffn_We, L1_ffn_be, L1_ffn_Wg, L1_ffn_bg):

    def _L0_attn_ref(queries, keys, values, Wq_w, Wq_b, Wk_w, Wk_b, Wv_w, Wv_b):
        import jax, jax.numpy as jnp
        import numpy as np
        B, S, H, NH = (1, 512, 128, 16)
        DH = H // NH

        def _split_heads(x):
            b, s, h = x.shape
            return jnp.transpose(x.reshape(b, s, NH, DH), (0, 2, 1, 3))
        q = jax.nn.relu(queries @ Wq_w.T + Wq_b)
        k = jax.nn.relu(keys @ Wk_w.T + Wk_b)
        v = jax.nn.relu(values @ Wv_w.T + Wv_b)
        qh, kh, vh = (_split_heads(q), _split_heads(k), _split_heads(v))
        score = jnp.einsum('bhsd,bhtd->bhst', qh, kh) / jnp.sqrt(jnp.float32(DH))
        attn = jax.nn.softmax(score, axis=-1)
        a = jnp.einsum('bhst,bhtd->bhsd', attn, vh)
        a = jnp.transpose(a, (0, 1, 3, 2)).reshape(q.shape[0], q.shape[1], q.shape[2])
        return a + queries

    def _L0_ffn_ref(x, w_gate_w, w_gate_b, W1, b1, W2, b2):
        import jax, jax.numpy as jnp
        import numpy as np
        TOPK = 2
        CAPACITY_FACTOR = 1.0
        EPS = 1e-06
        B, S, D = (4, 512, 128)
        E = 8
        SUB_H = 256 // E
        Bx, Sx, Dx = x.shape
        Ex = w_gate_b.shape[0]
        K = Sx // 2
        capacity = int(CAPACITY_FACTOR * Bx)
        gate_scores = jax.nn.softmax(x @ w_gate_w + w_gate_b, axis=-1)
        _, top_idx = jax.lax.top_k(gate_scores, TOPK)
        mask = jax.nn.one_hot(top_idx, Ex, dtype=gate_scores.dtype).sum(axis=-2)
        masked = gate_scores * mask
        denom = masked.sum(axis=0, keepdims=True) + EPS
        route = masked / denom * capacity
        route_eb = jnp.transpose(route, (2, 0, 1))
        _, seq_ids = jax.lax.top_k(route_eb, K)
        seq_ids = jnp.sort(seq_ids, axis=-1)
        xg = jax.vmap(lambda idx: jnp.take_along_axis(x, idx[..., None], axis=1))(seq_ids)
        h = jnp.einsum('ebkd,edh->ebkh', xg, W1) + b1[:, None, None, :]
        h = jax.nn.gelu(h, approximate=False)
        o = jnp.einsum('ebkh,ehd->ebkd', h, W2) + b2[:, None, None, :]
        flat_ids = (jnp.arange(Bx)[None, :, None] * Sx + seq_ids).reshape(-1)
        outs = jnp.zeros((Bx * Sx, Dx), x.dtype).at[flat_ids].add(o.reshape(-1, Dx))
        return outs.reshape(Bx, Sx, Dx)

    def _L1_attn_ref(x, W_qkv, q_scale, k_scale, W_out):
        import jax, jax.numpy as jnp
        import numpy as np
        D_MODEL = 128
        N_HEADS = 16
        LN_EPS = 1e-06

        def _layernorm(t, scale):
            mu = jnp.mean(t, axis=-1, keepdims=True)
            var = jnp.var(t, axis=-1, keepdims=True)
            return (t - mu) * jax.lax.rsqrt(var + LN_EPS) * scale
        B, S, D = x.shape
        H = N_HEADS
        Hd = D // H
        qkv = jnp.einsum('bsd,de->bse', x, W_qkv)
        q, k, v = jnp.split(qkv, 3, axis=-1)
        q = _layernorm(q, q_scale)
        k = _layernorm(k, k_scale)
        q = q.reshape(B, S, H, Hd)
        k = k.reshape(B, S, H, Hd)
        v = v.reshape(B, S, H, Hd)
        scores = jnp.einsum('bshd,bthd->bhst', q / jnp.sqrt(Hd).astype(q.dtype), k)
        future = jnp.triu(jnp.ones((S, S), dtype=bool), 1)
        scores = jnp.where(future[None, None, :, :], jnp.finfo(scores.dtype).min, scores)
        attn = jax.nn.softmax(scores, axis=-1)
        ctx = jnp.einsum('bhst,bthd->bshd', attn, v)
        out = jnp.einsum('bsd,de->bse', ctx.reshape(B, S, D), W_out)
        return out

    def _L1_ffn_ref(x, We, be, Wg, bg):
        import jax, jax.numpy as jnp
        import numpy as np
        B, S, D = (4, 256, 128)
        O = 128
        E = 8
        K = 2
        b, s, d = x.shape
        x_flat = x.reshape(-1, d)
        gates = jax.nn.softmax(x_flat @ Wg + bg, axis=-1)
        topk_gates, topk_idx = jax.lax.top_k(gates, K)
        topk_gates = topk_gates / jnp.sum(topk_gates, axis=1, keepdims=True)
        expert_out = jnp.einsum('nd,edo->neo', x_flat, We) + be
        selected = jnp.take_along_axis(expert_out, topk_idx[:, :, None], axis=1)
        out = jnp.sum(selected * topk_gates[:, :, None], axis=1)
        return out.reshape(b, s, -1)
    x = L0_attn_queries
    x = x + 0.5 * _L0_ffn_ref(_layernorm(x, axis=-1), L0_ffn_w_gate_w, L0_ffn_w_gate_b, L0_ffn_W1, L0_ffn_b1, L0_ffn_W2, L0_ffn_b2)
    x = x + _L0_attn_ref(_layernorm(x, axis=-1), L0_attn_keys, L0_attn_values, L0_attn_Wq_w, L0_attn_Wq_b, L0_attn_Wk_w, L0_attn_Wk_b, L0_attn_Wv_w, L0_attn_Wv_b)
    x = x + 0.5 * _L0_ffn_ref(_layernorm(x, axis=-1), L0_ffn_w_gate_w, L0_ffn_w_gate_b, L0_ffn_W1, L0_ffn_b1, L0_ffn_W2, L0_ffn_b2)
    x = x + 0.5 * _L1_ffn_ref(_layernorm(x, axis=-1), L1_ffn_We, L1_ffn_be, L1_ffn_Wg, L1_ffn_bg)
    x = x + _L1_attn_ref(_layernorm(x, axis=-1), L1_attn_W_qkv, L1_attn_q_scale, L1_attn_k_scale, L1_attn_W_out)
    x = x + 0.5 * _L1_ffn_ref(_layernorm(x, axis=-1), L1_ffn_We, L1_ffn_be, L1_ffn_Wg, L1_ffn_bg)
    return x

_drawn_inputs = setup_inputs


def setup_inputs(seed=0):
    import zlib

    import numpy as np

    out = dict(_drawn_inputs(seed))
    spreads = {'L0_ffn_w_gate_b': (0.0, 0.1),
     'L0_ffn_b1': (0.0, 0.474),
     'L0_ffn_b2': (0.0, 0.1),
     'L1_attn_q_scale': (1.0, 0.6),
     'L1_attn_k_scale': (1.0, 0.6)}
    factors = {'L0_attn_keys': 8.0,
     'L0_attn_values': 8.0,
     'L0_attn_Wq_w': 8.0,
     'L0_attn_Wq_b': 8.0,
     'L0_attn_Wk_w': 8.0,
     'L0_attn_Wk_b': 44.381,
     'L0_attn_Wv_w': 8.0,
     'L0_attn_Wv_b': 40.037,
     'L1_ffn_be': 14.45,
     'L1_ffn_bg': 4.97}
    for name, (base, spread) in spreads.items():
        noise = np.random.default_rng([zlib.crc32(name.encode()), seed]).standard_normal(out[name].shape)
        drawn = base * np.exp(spread * noise) if base else spread * noise
        out[name] = jnp.asarray(drawn.astype(out[name].dtype))
    for name, factor in factors.items():
        out[name] = (out[name] * factor).astype(out[name].dtype)
    return out
```

```python
from contextlib import ExitStack

import concourse.bass as bass
from concourse import mybir

ALU = mybir.AluOpType
ACT = mybir.ActivationFunctionType
F32 = mybir.dt.float32
BF16 = mybir.dt.bfloat16
U32 = mybir.dt.uint32
I32 = mybir.dt.int32
AX = mybir.AxisListType.X

P = 128
B, S, D = 2, 1024, 128
J = S // P
NT = B * J
E = 8
SUB = 32
KTOP = S // 2
NH, DH = 16, 8
TK = 512
CH = 512
NCH = B * S // CH
RB = 30
SHIFT_ROW = 9 * DH
ROWS = SHIFT_ROW + 3
NSLOT = 8
LEAD = 2
MASKED = -1e30


def attention_units(causal):
    return [(b, g, c) for b in range(B) for g in range(NH // 4) for c in range(S // CH)]


def max_items(unit, causal):
    _, _, c = unit
    items = []
    for st in range(CH // P):
        if not causal:
            items += [(st, i, 2, TK) for i in (0, 2)]
        elif c == 0:
            items += [(st, i, 2, P * (st + 1)) for i in (0, 2)]
        else:
            items += [(st, i, 1, CH + P * (st + 1)) for i in range(4)]
    return items


def exp_groups(unit, causal):
    _, _, c = unit
    if not causal:
        return [(tt, 0, False) for tt in range(TK // P)]
    return [(tt, max(0, P * tt - CH * c), P * tt >= CH * c) for tt in range((CH // P) * (c + 1))]


def macaron_kernel(nc, A, out):
    ctx = ExitStack()
    with ctx:
        def sb(name, shape, dt=F32):
            return ctx.enter_context(nc.sbuf_tensor(name, shape, dt))

        def sem(name):
            return ctx.enter_context(nc.semaphore(name))

        X = sb("X", [P, NT, D])
        XN = sb("XN", [P, NT, D])
        XT = sb("XT", [P, B * S])
        DEN = sb("DEN", [P, B * S])
        NUM = XT
        QSA = sb("QSA", [P, B * NH * S], BF16)
        QS = QSA[0:ROWS, :].rearrange("p (b h s) -> p b h s", b=B, h=NH)
        RAW = QSA[:, NH * S:2 * NH * S].bitcast(F32)[:, 0:NT * 2 * D].rearrange("p (n w d) -> p n w d", n=NT, w=2)
        KSB = sb("KSB", [P, 2 * NH * S], BF16)
        KS0 = KSB[0:ROWS, NH * TK:2 * NH * TK].rearrange("p (h t) -> p h t", h=NH)
        KS1 = KSB[0:ROWS, :].rearrange("p (b h t) -> p b h t", b=B, h=NH)
        HID = KSB[:, 0:NH * TK].bitcast(F32).rearrange("p (a t) -> p a t", a=2)
        PR = sb("PR", [P, NSLOT, CH])
        V1 = sb("V1", [P, NT, NH, 2 * DH])
        V0 = V1[:, 0:TK // P]
        QF = PR[:, 0:2, :]
        RES = PR[:, 2, :]
        PARTS = PR[:, 3:6, :].rearrange("p a c -> p (a c)").bitcast(BF16).rearrange("p (w q c) -> p w q c", w=2, q=3)
        OG = sb("OG", [P, 2, CH])
        MX = sb("MX", [P, 2, 4, 4])
        MR = sb("MR", [P, 4, 4])
        MP = sb("MP", [P, 2, 4, 12], BF16)
        MT = KSB[96:108, 0:2 * CH].rearrange("p (a c) -> p a c", a=2)
        T8 = DEN[0:E, :]
        T8B = PR[0:E, 6:8, :].rearrange("p a c -> p (a c)").bitcast(BF16)

        ident = sb("ident", [P, P])
        identb = sb("identb", [P, P], BF16)
        onesb = sb("onesb", [P, P], BF16)
        trib = sb("trib", [P, P], BF16)
        maskb = sb("maskb", [P, P], BF16)
        expandb = sb("expandb", [E, 2 * P], BF16)
        prio = sb("prio", [P, E])

        Wg0 = sb("Wg0", [P, E])
        Wg1 = sb("Wg1", [P, E])
        gb0 = sb("gb0", [P, E])
        gb1 = sb("gb1", [P, E])
        W1 = sb("W1", [P, E, SUB])
        b1c = sb("b1c", [P, 2])
        W2 = sb("W2", [P, 2, D])
        b2r = sb("b2r", [E, D])
        We = sb("We", [P, E, D])
        ber = sb("ber", [E, D])
        Wqkv = PR[:, 7, 0:3 * D]
        Wo = sb("Wo", [P, D])
        qsc = sb("qsc", [P, 1])
        ksc = sb("ksc", [P, 1])
        Wraw = XT[:, 0:3 * D].rearrange("p (w d) -> p w d", w=3)
        bvr = XT[:, 3 * D:4 * D]
        KVraw = XT[:, 2 * CH:4 * CH].rearrange("p (a c) -> p a c", a=2)
        WT = OG[:, 0, 0:3 * D].rearrange("p (w d) -> p w d", w=3)
        bqc = sb("bqc", [P, 1])
        bkc = sb("bkc", [P, 1])
        KVT = DEN[:, 0:2 * TK].rearrange("p (a t) -> p a t", a=2)

        st6 = sb("st6", [P, NT, 6])
        mv = sb("mv", [P, NT, 2])
        rstd = sb("rstd", [P, NT])
        st6b = OG[:, 1, 0:12 * J].rearrange("p (n w c) -> p n w c", n=J, w=2)
        mvb = OG[:, 1, 12 * J:16 * J].rearrange("p (n w c) -> p n w c", n=J, w=2)
        rsb = OG[:, 1, 16 * J:18 * J].rearrange("p (n w) -> p n w", n=J)
        RQ = OG[:, 1, 3 * P:3 * P + 3 * NT].rearrange("p (a n) -> p a n", a=3)
        QKN = PR[:, 6, :].rearrange("p (n w d) -> p n w d", n=2, w=2)
        G, G2, GE, EQ = (OG[:, 1, i * NT * E:(i + 1) * NT * E].rearrange("p (n e) -> p n e", e=E) for i in range(4))
        SEL = sb("SEL", [P, NT, E])
        r16 = sb("r16", [P, NT])
        den8 = PR[:, 0, P:P + J * E].rearrange("p (j e) -> p j e", j=J)
        RT = OG[:, 0, 3 * D:4 * D].rearrange("p (b e j) -> p b e j", b=B, e=E)
        PT = PR[:, 0, 0:NT * E].rearrange("p (b e j) -> p b e j", b=B, e=E)
        CA, CB = (PR[:, 1 + i, 0:NT * E // 2].bitcast(BF16).rearrange("p (b e j) -> p b e j", b=B, e=E) for i in range(2))
        thr = sb("thr", [P, NT])
        cand = sb("cand", [P, NT])
        took = sb("took", [P, NT])

        scrA = nc.dram_tensor("scr_k0", [P, 3, TK], BF16, kind="Internal").ap()
        scrQ0 = nc.dram_tensor("scr_q0", [P, 3, B * S], BF16, kind="Internal").ap()
        scrQ1 = nc.dram_tensor("scr_q1", [P, 3, B * S], BF16, kind="Internal").ap()
        scrK1 = nc.dram_tensor("scr_k1", [P, 3, B * S], BF16, kind="Internal").ap()

        PS = [ctx.enter_context(nc.psum_tensor(f"PS{i}", [P, 2 * CH], F32)) for i in range(4)]

        def bank(i):
            return PS[i // 2][:, (i % 2) * CH:(i % 2 + 1) * CH]

        sems = {}

        def sm(name):
            if name not in sems:
                sems[name] = sem(name)
            return sems[name]

        block = ctx.enter_context(nc.Block())

        def shift_item(a, u):
            units = attention_units(a)
            n = sum(len(max_items(un, a)) + 1 for un in units[:u + 1])
            return n + 1 if u + 1 < len(units) else n - 1

        N_CONST = 4 + 1 + 1 + E + 1

        @block.sync
        def _(sp):
            def load(dst, src, s):
                sp.dma_start(dst, src).then_inc(sm(s), 16)

            for b in range(B):
                load(X[:, b * J:(b + 1) * J, :], A["L0_attn_queries"][b].rearrange("(p j) d -> p j d", j=J), f"x_in{b}")
            load(Wraw[:, 0, :], A["L0_attn_Wq_w"], "kv_in")
            load(Wraw[:, 1, :], A["L0_attn_Wk_w"], "kv_in")
            load(Wraw[:, 2, :], A["L0_attn_Wv_w"], "kv_in")
            load(KVraw[:, 0, :].rearrange("p (t d) -> p t d", d=D), A["L0_attn_keys"][0].rearrange("(t p) d -> p t d", p=P), "kv_in")
            load(KVraw[:, 1, :].rearrange("p (t d) -> p t d", d=D), A["L0_attn_values"][0].rearrange("(t p) d -> p t d", p=P), "kv_in")
            load(bqc[:, :], A["L0_attn_Wq_b"].rearrange("(p o) -> p o", o=1), "kv_in")
            load(bkc[:, :], A["L0_attn_Wk_b"].rearrange("(p o) -> p o", o=1), "kv_in")
            load(bvr[:, :], A["L0_attn_Wv_b"].rearrange("(o d) -> o d", o=1).to_broadcast([P, D]), "kv_in")
            load(Wg0[:, :], A["L0_ffn_w_gate_w"], "f0_in")
            load(gb0[:, :], A["L0_ffn_w_gate_b"].rearrange("(o d) -> o d", o=1).to_broadcast([P, E]), "f0_in")
            load(W1[:, :, :], A["L0_ffn_W1"].rearrange("e d h -> d e h"), "f0_in")
            for a in range(2):
                load(b1c[:, a:a + 1], A["L0_ffn_b1"][4 * a:4 * a + 4].rearrange("e h -> (e h)").rearrange("(p o) -> p o", o=1), "f0_in")
            load(W2[:, :, :], A["L0_ffn_W2"].rearrange("e h d -> (e h) d").rearrange("(a p) d -> p a d", p=P), "f0_in")
            load(b2r[:, :], A["L0_ffn_b2"], "f0_in")
            load(Wg1[:, :], A["L1_ffn_Wg"], "f1_in")
            load(gb1[:, :], A["L1_ffn_bg"].rearrange("(o d) -> o d", o=1).to_broadcast([P, E]), "f1_in")
            load(We[:, :, :], A["L1_ffn_We"].rearrange("e d o -> d e o"), "f1_in")
            load(ber[:, :], A["L1_ffn_be"], "f1_in")
            load(Wo[:, :], A["L1_attn_W_out"], "a1_in")
            load(qsc[:, :], A["L1_attn_q_scale"].rearrange("(p o) -> p o", o=1), "a1_in")
            load(ksc[:, :], A["L1_attn_k_scale"].rearrange("(p o) -> p o", o=1), "a1_in")

            def stack(dst, scr, by_part, s):
                for a in range(3):
                    for c in range(3):
                        r = DH * (3 * a + c)
                        load(dst[r:r + DH], scr.rearrange("(h d) q s -> d q h s", h=NH)[:, a if by_part else c], s)

            def attention_dma(a):
                scr = [scrQ0, scrQ1][a]
                for b in range(B):
                    for c in range(2 * b, 2 * b + 2):
                        if a == 0:
                            sp.wait_ge(sm("parts0"), c + 1)
                            load(scr[:, :, c * CH:(c + 1) * CH], PARTS[:, c % 2, :, :], f"scr0_{c}")
                        else:
                            sp.wait_ge(sm("parts1"), 2 * c + 1)
                            load(scrQ1[:, :, c * CH:(c + 1) * CH], PARTS[:, 0, :, :], f"scr1_{2 * c}")
                            sp.wait_ge(sm("parts1"), 2 * c + 2)
                            load(scrK1[:, :, c * CH:(c + 1) * CH], PARTS[:, 1, :, :], f"scr1_{2 * c + 1}")
                    n = 2 * (a + 1)
                    for c in range(n * b, n * b + n):
                        sp.wait_ge(sm(f"scr{a}_{c}"), 16)
                    stack(QS[:, b, :, :], scr[:, :, b * S:(b + 1) * S], True, f"qstack{a}_{b}")
                    if a == 1:
                        sp.wait_ge(sm("ks_ones"), 2)
                        stack(KS1[:, b, :, :], scrK1[:, :, b * S:(b + 1) * S], False, f"kstack{b}")
                units = attention_units(a)

                def shift_rows(u):
                    b, g, c = units[u]
                    sp.wait_ge(sm(f"mxfree{a}"), shift_item(a, u) + 1)
                    for q in range(3):
                        load(QS[SHIFT_ROW + q:SHIFT_ROW + q + 1, b, 4 * g:4 * g + 4, c * CH:(c + 1) * CH],
                             MT[4 * q:4 * q + 4, u % 2, :], f"mrow{a}_{u % 2}")

                def heads_out(u):
                    b, g, c = units[u]
                    sp.wait_ge(sm(f"og{a}"), u + 1)
                    cols = slice(b * S + c * CH, b * S + (c + 1) * CH)
                    for i in range(4):
                        h = 4 * g + i
                        load(NUM[DH * h:DH * h + DH, cols], OG[32 * i:32 * i + DH, u % 2, :], f"ogout{a}_{u % 2}")
                        load(DEN[DH * h:DH * h + DH, cols], OG[32 * i + DH:32 * i + 2 * DH, u % 2, :], f"ogout{a}_{u % 2}")

                for u in range(LEAD):
                    shift_rows(u)
                for u in range(len(units)):
                    if u >= 1:
                        heads_out(u - 1)
                    if u + LEAD < len(units):
                        shift_rows(u + LEAD)
                heads_out(len(units) - 1)

            sp.wait_ge(sm("k0_parts"), 1)
            load(scrA, PARTS[:, 0, :, :], "k0_scr")
            sp.wait_ge(sm("k0_scr"), 16)
            sp.wait_ge(sm("ks_ones"), 1)
            stack(KS0, scrA, False, "k0_stack")
            attention_dma(0)
            sp.wait_ge(sm("xadd2"), NCH)
            load(Wqkv, A["L1_attn_W_qkv"], "wqkv_in")
            attention_dma(1)
            for b in range(B):
                sp.wait_ge(sm("xadd5"), NCH // B * (b + 1))
                load(out[b].rearrange("(p j) d -> p j d", j=J), X[:, b * J:(b + 1) * J, :], "stored")
            sp.wait_ge(sm("stored"), 16 * B)

        @block.gpsimd
        def _(pool):
            pool.memset(ident[:, :], 0.0).then_inc(sm("c_set"), 1)
            pool.memset(identb[:, :], 0.0).then_inc(sm("c_set"), 1)
            pool.memset(trib[:, :], 1.0).then_inc(sm("c_set"), 1)
            pool.memset(maskb[:, :], MASKED).then_inc(sm("c_set"), 1)
            pool.memset(expandb[:, :], 1.0).then_inc(sm("c_set"), 1)
            pool.wait_ge(sm("c_set"), 5)
            for m in (ident, identb):
                pool.affine_select(out=m[:, :], in_=m[:, :], compare_op=ALU.not_equal, fill=1.0, base=0,
                                   pattern=[[-1, P]], channel_multiplier=1).then_inc(sm("consts"), 1)
            pool.affine_select(out=trib[:, :], in_=trib[:, :], compare_op=ALU.is_gt, fill=0.0, base=0,
                               pattern=[[1, P]], channel_multiplier=-1).then_inc(sm("consts"), 1)
            pool.affine_select(out=maskb[:, :], in_=maskb[:, :], compare_op=ALU.is_gt, fill=0.0, base=0,
                               pattern=[[1, P]], channel_multiplier=-1).then_inc(sm("consts"), 1)
            pool.affine_select(out=expandb[:, :], in_=expandb[:, :], compare_op=ALU.is_ge, fill=0.0, base=0,
                               pattern=[[1, 2 * P]], channel_multiplier=-SUB).then_inc(sm("c_set"), 1)
            pool.wait_ge(sm("c_set"), 6)
            pool.affine_select(out=expandb[:, :], in_=expandb[:, :], compare_op=ALU.is_ge, fill=0.0, base=SUB - 1,
                               pattern=[[-1, 2 * P]], channel_multiplier=SUB).then_inc(sm("consts"), 1)
            pool.memset(onesb[:, :], 1.0).then_inc(sm("consts"), 1)
            for e in range(E):
                pool.memset(prio[:, e:e + 1], float(E - e)).then_inc(sm("consts"), 1)
            pool.wait_ge(sm("consts"), 4 + 1 + 1 + E)
            pool.memset(KSB[64:96, NH * TK:2 * NH * TK], 1.0).then_inc(sm("ks_ones"), 1)
            pool.wait_ge(sm("ks_ones"), 1)
            pool.memset(V1[:, :, :, DH:2 * DH], 1.0).then_inc(sm("consts"), 1)

            pool.wait_ge(sm("consts"), N_CONST)
            pool.wait_ge(sm("xadd2"), NCH)
            pool.memset(KSB[64:96, :], 1.0).then_inc(sm("ks_ones"), 1)
            pool.wait_ge(sm("ks_ones"), 2)
            n = 0
            for unit in attention_units(1):
                for tt, off, diag in exp_groups(unit, True):
                    for i in range(4):
                        if diag:
                            pool.wait_ge(sm("p1"), n + 1)
                            blk = PR[:, n % NSLOT, off:off + P]
                            pool.affine_select(out=blk, in_=blk, compare_op=ALU.is_ge, fill=0.0, base=0,
                                               pattern=[[1, P]], channel_multiplier=-1).then_inc(sm("pmask"), 1)
                        n += 1


        @block.tensor
        def _(pe):
            def transpose_x(k):
                for n in range(NT):
                    q = n // 4
                    pe.wait_ge(sm(f"xn{k}"), n + 1)
                    if q >= 2 and n % 4 == 0:
                        pe.wait_ge(sm(f"xt{k}"), q - 1)
                    pe.transpose(bank(q % 2)[:, (n % 4) * P:(n % 4 + 1) * P], XN[:, n, :], ident[:, :])\
                        .then_inc(sm(f"xtp{k}"), 1)

            def gates(k, Wg):
                for n in range(NT):
                    pe.wait_ge(sm(f"xt{k}"), n // 4 + 1)
                    mm = pe.matmul(bank(2)[:, n * E:(n + 1) * E], XT[:, n * P:(n + 1) * P], Wg[:, :], start=True, stop=True)
                mm.then_inc(sm(f"lg{k}"), 1)

            def transpose_sel(k):
                pe.wait_ge(sm(f"sel{k}"), 2 if k in (0, 2) else 1)
                for n in range(NT):
                    q = n // 4
                    if q >= 2 and n % 4 == 0:
                        pe.wait_ge(sm(f"t8{k}"), q - 1)
                    mm = pe.transpose(bank(q % 2)[0:E, (n % 4) * P:(n % 4 + 1) * P], SEL[:, n, :], ident[:, :])
                    if n % 4 == 3:
                        mm.then_inc(sm(f"t8p{k}"), 1)

            def ffn0(k):
                transpose_x(k)
                pe.wait_ge(sm("f0_in"), 16 * 7)
                gates(k, Wg0)
                n = 0
                for q in range(NCH):
                    for a in range(2):
                        if n >= 4:
                            pe.wait_ge(sm(f"hid{k}"), n - 3)
                        pe.matmul(bank(4 + n % 4), W1[:, 4 * a:4 * a + 4, :].rearrange("p e h -> p (e h)"),
                                  XT[:, q * CH:(q + 1) * CH], start=True, stop=True).then_inc(sm(f"hidp{k}"), 1)
                        n += 1
                for r in range(RB):
                    pe.wait_ge(sm(f"cmp{k}"), r + 1)
                    for j in range(J):
                        mm = pe.matmul(bank(3)[:, 0:NT], onesb[:, :], CA[:, :, :, j].rearrange("p b e -> p (b e)"),
                                       start=(j == 0), stop=(j == J - 1))
                    mm.then_inc(sm(f"cnt{k}"), 1)
                pe.wait_ge(sm(f"gteq{k}"), 2)
                rank = bank(3)[:, 0:NT * J].rearrange("p (n j) -> p n j", j=J)
                for j in range(J):
                    gt = CA[:, :, :, j].rearrange("p b e -> p (b e)").unsqueeze(2).to_broadcast([P, NT, J])
                    eq = CB[:, :, :, j].rearrange("p b e -> p (b e)").unsqueeze(2)
                    pe.matmul(rank, onesb[:, :], gt, start=(j == 0), stop=False)
                    mm = pe.matmul(rank, trib[:, :], eq.to_broadcast([P, NT, J]), start=False, stop=(j == J - 1))
                    if j < J - 1:
                        pe.matmul(rank[:, :, j + 1:J], identb[:, :], eq.to_broadcast([P, NT, J - 1 - j]),
                                  start=False, stop=False)
                mm.then_inc(sm(f"rank{k}"), 1)
                transpose_sel(k)
                n = 0
                for q in range(NCH):
                    pe.wait_ge(sm(f"t8b{k}"), q + 1)
                    for a in range(2):
                        if n >= 4:
                            pe.wait_ge(sm(f"hm{k}"), n - 3)
                        pe.matmul(bank(4 + n % 4), expandb[:, a * P:(a + 1) * P], T8B[:, q * CH:(q + 1) * CH],
                                  start=True, stop=True).then_inc(sm(f"spread{k}"), 1)
                        n += 1
                for n in range(NT):
                    q = n // 4
                    if n % 4 == 0:
                        pe.wait_ge(sm(f"hm{k}"), 2 * q + 2)
                        pe.wait_ge(sm(f"t8{k}"), q + 1)
                        if q >= 2:
                            pe.wait_ge(sm(f"xadd{k}"), q - 1)
                    dst = bank(2 + q % 2)[:, (n % 4) * P:(n % 4 + 1) * P]
                    cols = slice(n * P, (n + 1) * P)
                    pe.matmul(dst, HID[:, 0, cols], W2[:, 0, :], start=True, stop=False)
                    pe.matmul(dst, HID[:, 1, cols], W2[:, 1, :], start=False, stop=False)
                    pe.matmul(dst, T8[:, cols], b2r[:, :], start=False, stop=True).then_inc(sm(f"y{k}"), 1)

            def ffn1(k):
                transpose_x(k)
                if k == 3:
                    pe.wait_ge(sm("f1_in"), 16 * 4)
                gates(k, Wg1)
                for n in range(NT):
                    if n >= 2:
                        pe.wait_ge(sm(f"comb{k}"), n - 1)
                    for a in range(2):
                        mm = pe.matmul(bank(4 + 2 * (n % 2) + a), XT[:, n * P:(n + 1) * P],
                                       We[:, 4 * a:4 * a + 4, :].rearrange("p e o -> p (e o)"), start=True, stop=True)
                    mm.then_inc(sm(f"ye{k}"), 1)
                    if n == 1:
                        transpose_sel(k)
                for n in range(NT):
                    q = n // 4
                    if n % 4 == 0:
                        pe.wait_ge(sm(f"t8{k}"), q + 1)
                        if q >= 2:
                            pe.wait_ge(sm(f"xadd{k}"), q - 1)
                    pe.matmul(bank(2 + q % 2)[:, (n % 4) * P:(n % 4 + 1) * P], T8[:, n * P:(n + 1) * P], ber[:, :],
                              start=True, stop=True).then_inc(sm(f"y{k}"), 1)

            def keys_values():
                pe.wait_ge(sm("consts"), N_CONST)
                pe.wait_ge(sm("kv_in"), 16 * 8)
                for w in range(3):
                    mm = pe.transpose(bank(0)[:, w * P:(w + 1) * P], Wraw[:, w, :], ident[:, :])
                mm.then_inc(sm("wtp"), 1)
                for a in range(2):
                    for t in range(4):
                        mm = pe.transpose(bank(1 + a)[:, t * P:(t + 1) * P], KVraw[:, a, t * P:(t + 1) * P], ident[:, :])
                    mm.then_inc(sm("wtp"), 1)
                pe.wait_ge(sm("wt"), 2)
                pe.matmul(bank(3), WT[:, 1, :], KVT[:, 0, :], start=True, stop=True).then_inc(sm("kp"), 1)
                pe.wait_ge(sm("wt"), 3)
                for t in range(4):
                    mm = pe.matmul(bank(4)[:, t * P:(t + 1) * P], KVT[:, 1, t * P:(t + 1) * P], WT[:, 2, :],
                                   start=True, stop=True)
                mm.then_inc(sm("vp"), 1)

            def attention(a, k):
                units = attention_units(a)
                transpose_x(k)
                if a == 0:
                    for c in range(NCH):
                        pe.wait_ge(sm(f"xt{k}"), NCH if c < 2 else NCH)
                        if c >= 2:
                            pe.wait_ge(sm("qf0"), c - 1)
                        pe.matmul(bank(4 + c % 2), WT[:, 0, :], XT[:, c * CH:(c + 1) * CH], start=True, stop=True)\
                            .then_inc(sm("qp0"), 1)
                    pe.wait_ge(sm("k0_stack"), 16 * 9)
                else:
                    pe.wait_ge(sm("a1_in"), 16 * 3)
                    pe.wait_ge(sm("wqkv_in"), 16)
                    pe.wait_ge(sm(f"xt{k}"), NCH)
                    for b in range(B + 1):
                        for n in range(b * J, (b + 1) * J) if b < B else ():
                            if n >= 2:
                                pe.wait_ge(sm("v1"), 2 * (n - 1))
                            pe.matmul(bank(4 + n % 2)[:, 0:3 * D], XT[:, n * P:(n + 1) * P], Wqkv,
                                      start=True, stop=True).then_inc(sm("qkvp"), 1)
                        for m in range((b - 1) * J, b * J) if b > 0 else ():
                            pe.wait_ge(sm("qkn"), 2 * (m + 1))
                            if m % 4 == 0 and m >= 4:
                                pe.wait_ge(sm("qkt"), 2 * (m // 4))
                            for w in range(2):
                                mm = pe.transpose(bank(6 + w)[:, (m % 4) * P:(m % 4 + 1) * P], QKN[:, m % 2, w, :], ident[:, :])
                            mm.then_inc(sm("qktp"), 1)

                KSof = (lambda b: KS0) if a == 0 else (lambda b: KS1[:, b])
                Vof = (lambda b, tt: V0[:, tt]) if a == 0 else (lambda b, tt: V1[:, b * J + tt])
                state = {"mx": 0, "sc": 0, "pv": 0, "diag": 0}

                def row_max(u, item):
                    b, g, c = units[u]
                    st, i0, nh, w = item
                    m = state["mx"]
                    if m >= 2:
                        pe.wait_ge(sm(f"mxfree{a}"), m - 1)
                    dst = PS[m % 2]
                    s0 = c * CH + st * P
                    for i in range(i0, i0 + nh):
                        q = QS[0:SHIFT_ROW, b, 4 * g + i, s0:s0 + P]
                        for t0 in range(0, w, CH):
                            t1 = min(w, t0 + CH)
                            o = (i - i0) * CH + t0
                            last = bool(a) and t1 == w
                            mm = pe.matmul(dst[:, o:o + t1 - t0], q, KSof(b)[0:SHIFT_ROW, 4 * g + i, t0:t1],
                                           start=True, stop=not last)
                            if last:
                                mm = pe.matmul(dst[:, o + t1 - t0 - P:o + t1 - t0], identb[:, :], maskb[:, :],
                                               start=False, stop=True)
                    mm.then_inc(sm(f"mxp{a}"), 1)
                    state["mx"] += 1

                def transpose_shift(u):
                    m = state["mx"]
                    pe.wait_ge(sm(f"mxfree{a}"), m - 1)
                    pe.wait_ge(sm(f"mp{a}"), u + 1)
                    dst = PS[m % 2][0:12, 0:CH // 2].bitcast(BF16)
                    for st in range(4):
                        mm = pe.transpose(dst[:, st * P:(st + 1) * P], MP[:, u % 2, st, :], identb[:, :])
                    mm.then_inc(sm(f"mxp{a}"), 1)
                    state["mx"] += 1

                def max_stream():
                    for u in range(len(units)):
                        for n, item in enumerate(max_items(units[u], a)):
                            if n == 2 and u >= 1:
                                yield lambda u=u: transpose_shift(u - 1)
                            yield lambda u=u, item=item: row_max(u, item)
                    yield lambda: transpose_shift(len(units) - 1)

                def scores(u, tt, off):
                    b, g, c = units[u]
                    for i in range(4):
                        n = state["sc"]
                        if n >= 2:
                            pe.wait_ge(sm(f"p{a}"), n - 1)
                        s0 = c * CH + off
                        pe.matmul(bank(4 + n % 2)[:, 0:CH - off], KSof(b)[0:ROWS, 4 * g + i, tt * P:(tt + 1) * P],
                                  QS[0:ROWS, b, 4 * g + i, s0:(c + 1) * CH], start=True, stop=True)\
                            .then_inc(sm(f"sc{a}"), 1)
                        state["sc"] += 1

                def values(u, tt, off, diag, first, last):
                    b, g, c = units[u]
                    if first and u >= 2:
                        pe.wait_ge(sm(f"og{a}"), u - 1)
                    for i in range(4):
                        n = state["pv"]
                        if a == 1 and diag:
                            pe.wait_ge(sm("pmask"), state["diag"] + 1)
                            state["diag"] += 1
                        else:
                            pe.wait_ge(sm(f"p{a}"), n + 1)
                        pe.matmul(bank(6 + u % 2)[32 * i:32 * i + 2 * DH, off:CH], Vof(b, tt)[:, 4 * g + i, :],
                                  PR[:, n % NSLOT, off:CH], start=first, stop=last).then_inc(sm(f"pv{a}"), 1)
                        state["pv"] += 1

                stream = max_stream()
                loaded = [False, False]

                def need_stack(b):
                    if not loaded[b]:
                        loaded[b] = True
                        pe.wait_ge(sm(f"qstack{a}_{b}"), 16 * 9)
                        if a == 1:
                            pe.wait_ge(sm(f"kstack{b}"), 16 * 9)

                per_unit = [len(max_items(un, a)) + 1 for un in units]
                need_stack(0)
                lead = sum(per_unit[:LEAD]) + 2
                for _ in range(lead):
                    next(stream)()
                total = sum(per_unit)
                done = lead
                target = 0
                pending = None
                for u, unit in enumerate(units):
                    pe.wait_ge(sm(f"mrow{a}_{u % 2}"), 48 * (u // 2 + 1))
                    groups = exp_groups(unit, a)
                    if u + LEAD < len(units) and units[u + LEAD][0] == 1:
                        need_stack(1)
                    goal = min(total, sum(per_unit[:u + LEAD + 1]) + 2)
                    start_done = done
                    for k2, (tt, off, diag) in enumerate(groups):
                        scores(u, tt, off)
                        upto = start_done + (goal - start_done) * (k2 + 1) // len(groups)
                        while done < upto:
                            next(stream)()
                            done += 1
                        if pending:
                            values(*pending)
                        pending = (u, tt, off, diag, k2 == 0, k2 == len(groups) - 1)
                values(*pending)
                if a == 1:
                    for n in range(NT):
                        q = n // 4
                        if n % 4 == 0:
                            pe.wait_ge(sm("ctx"), q // 2 + 1)
                            if q >= 2:
                                pe.wait_ge(sm(f"xadd{k}"), q - 1)
                        b, j = n // J, n % J
                        pe.matmul(bank(q % 2)[:, (n % 4) * P:(n % 4 + 1) * P],
                                  NUM[:, b * S:(b + 1) * S].rearrange("p (s j) -> p j s", j=J)[:, j, :], Wo[:, :],
                                  start=True, stop=True).then_inc(sm(f"y{k}"), 1)

            keys_values()
            ffn0(0)
            attention(0, 1)
            ffn0(2)
            ffn1(3)
            attention(1, 4)
            ffn1(5)

        @block.scalar
        def _(act):
            def copy_xt(k, natural):
                for q in range(NCH):
                    act.wait_ge(sm(f"xtp{k}"), 4 * q + 4)
                    if natural:
                        b, j0 = q // 2, 4 * (q % 2)
                        dst = XT[:, b * S:(b + 1) * S].rearrange("d (p j) -> d j p", j=J)[:, j0:j0 + 4, :]
                        src = bank(q % 2).rearrange("d (j p) -> d j p", p=P)
                    else:
                        dst, src = XT[:, q * CH:(q + 1) * CH], bank(q % 2)
                    act.activation(dst, src, ACT.Copy).then_inc(sm(f"xt{k}"), 1)

            def gate_exp(k):
                act.wait_ge(sm(f"gsub{k}"), 1)
                act.activation(GE, G, ACT.Exp).then_inc(sm(f"gexp{k}"), 1)

            def copy_t8(k):
                for q in range(NCH):
                    act.wait_ge(sm(f"t8p{k}"), q + 1)
                    act.activation(T8[:, q * CH:(q + 1) * CH], bank(q % 2)[0:E, :], ACT.Copy).then_inc(sm(f"t8{k}"), 1)

            def ffn0(k):
                copy_xt(k, False)
                gate_exp(k)
                n = 0
                for q in range(NCH):
                    for a in range(2):
                        act.wait_ge(sm(f"hidp{k}"), n + 1)
                        act.activation(HID[:, a, q * CH:(q + 1) * CH], bank(4 + n % 4), ACT.Gelu, bias=b1c[:, a:a + 1])\
                            .then_inc(sm(f"hid{k}"), 1)
                        n += 1
                copy_t8(k)

            def ffn1(k):
                copy_xt(k, False)
                gate_exp(k)
                copy_t8(k)

            def attention(a, k):
                units = attention_units(a)
                copy_xt(k, True)
                if a == 0:
                    for c in range(NCH):
                        act.wait_ge(sm("qp0"), c + 1)
                        if c >= 2:
                            act.wait_ge(sm("parts0"), c - 1)
                        act.activation(QF[:, c % 2, :], bank(4 + c % 2), ACT.Relu, bias=bqc[:, 0:1]).then_inc(sm("qf0"), 1)
                else:
                    for n in range(NT):
                        act.wait_ge(sm("qkvp"), n + 1)
                        act.activation(V1[:, n, :, 0:DH], bank(4 + n % 2)[:, 2 * D:3 * D].rearrange("p (h d) -> p h d", h=NH),
                                       ACT.Copy).then_inc(sm("v1"), 1)
                        act.activation(RAW[:, n], bank(4 + n % 2)[:, 0:2 * D].rearrange("p (w d) -> p w d", w=2), ACT.Copy)\
                            .then_inc(sm("v1"), 1)
                n = 0

                def sums_out(u):
                    act.wait_ge(sm(f"pv{a}"), 4 * sum(len(exp_groups(un, a)) for un in units[:u + 1]))
                    if u >= 2:
                        act.wait_ge(sm(f"ogout{a}_{u % 2}"), 128 * (u // 2))
                    act.activation(OG[:, u % 2, :], bank(6 + u % 2), ACT.Copy).then_inc(sm(f"og{a}"), 1)

                for u, unit in enumerate(units):
                    for k2, (tt, off, diag) in enumerate(exp_groups(unit, a)):
                        for i in range(4):
                            act.wait_ge(sm(f"sc{a}"), n + 1)
                            if n >= NSLOT:
                                act.wait_ge(sm(f"pv{a}"), n - NSLOT + 1)
                            act.activation(PR[:, n % NSLOT, off:CH], bank(4 + n % 2)[:, 0:CH - off], ACT.Exp)\
                                .then_inc(sm(f"p{a}"), 1)
                            n += 1
                        if k2 == 1 and u >= 1:
                            sums_out(u - 1)
                sums_out(len(units) - 1)

            act.wait_ge(sm("wtp"), 1)
            act.activation(WT[:, :, :].rearrange("p w d -> p (w d)"), bank(0)[:, 0:3 * P], ACT.Copy).then_inc(sm("wt"), 1)
            for a in range(2):
                act.wait_ge(sm("wtp"), 2 + a)
                act.activation(KVT[:, a, :], bank(1 + a), ACT.Copy).then_inc(sm("wt"), 1)
            act.wait_ge(sm("kp"), 1)
            act.activation(QF[:, 0, :], bank(3), ACT.Relu, bias=bkc[:, 0:1]).then_inc(sm("kf"), 1)
            ffn0(0)
            attention(0, 1)
            ffn0(2)
            ffn1(3)
            attention(1, 4)
            ffn1(5)

        @block.vector
        def _(dve):
            chain = [0]

            def link(ins):
                chain[0] += 1
                ins.then_inc(sm("dve_chain"), 1)
                dve.wait_ge(sm("dve_chain"), chain[0])

            def mark(ins):
                chain[0] += 1
                ins.then_inc(sm("dve_chain"), 1)

            def settle():
                dve.wait_ge(sm("dve_chain"), chain[0])

            def rsqrt(dst, src, eps):
                a, y, t = RQ[:, 0, :], RQ[:, 1, :], RQ[:, 2, :]
                link(dve.tensor_scalar(a, src, eps, None, ALU.add))
                link(dve.tensor_scalar(t.bitcast(I32), a.bitcast(I32), 1, None, ALU.logical_shift_right))
                link(dve.tensor_scalar(y.bitcast(I32), t.bitcast(I32), -1.0, float(0x5f3759df), ALU.mult, ALU.add))
                for step in range(3):
                    link(dve.scalar_tensor_tensor(out=t, in0=y, scalar=-0.5, in1=y, op0=ALU.mult, op1=ALU.mult))
                    link(dve.tensor_tensor(t, t, a, ALU.mult))
                    link(dve.scalar_tensor_tensor(out=(dst if step == 2 else y), in0=t, scalar=1.5, in1=y,
                                                  op0=ALU.add, op1=ALU.mult))

            def layernorm(k):
                settle()
                for n in range(NT):
                    if k == 0 and n % J == 0:
                        dve.wait_ge(sm(f"x_in{n // J}"), 16)
                    mark(dve.bn_stats(st6[:, n, :], X[:, n, :]))
                settle()
                for n in range(NT):
                    mark(dve.bn_aggr(mv[:, n, :], st6[:, n, :]))
                settle()
                rsqrt(rstd[:, :], mv[:, :, 1], 1e-5)
                for n in range(NT):
                    dve.tensor_scalar(XN[:, n, :], X[:, n, :], mv[:, n, 0:1], rstd[:, n:n + 1], ALU.subtract, ALU.mult)\
                        .then_inc(sm(f"xn{k}"), 1)
                dve.wait_ge(sm(f"xn{k}"), NT)

            def wide(t):
                return t[:, :].unsqueeze(2).to_broadcast([P, NT, E])

            def gate_top2(k, gb):
                pri = prio[:, :].unsqueeze(1).to_broadcast([P, NT, E])
                logits = bank(2)[:, 0:NT * E].rearrange("p (n e) -> p n e", e=E)
                dve.wait_ge(sm(f"lg{k}"), 1)
                link(dve.tensor_tensor(G, logits, gb[:, :].unsqueeze(1).to_broadcast([P, NT, E]), ALU.add))
                link(dve.tensor_reduce(r16[:, :], G, AX, ALU.max))
                dve.tensor_tensor(G, G, wide(r16), ALU.subtract).then_inc(sm(f"gsub{k}"), 1)
                dve.wait_ge(sm(f"gexp{k}"), 1)
                link(dve.tensor_reduce(r16[:, :], GE, AX, ALU.add))
                link(dve.reciprocal(r16[:, :], r16[:, :]))
                link(dve.tensor_tensor(G, GE, wide(r16), ALU.mult))
                src = G
                for turn in range(2):
                    link(dve.tensor_reduce(r16[:, :], src[:, :, :], AX, ALU.max))
                    link(dve.tensor_tensor(EQ, src[:, :, :], wide(r16), ALU.is_equal))
                    link(dve.tensor_tensor(EQ, EQ, pri, ALU.mult))
                    link(dve.tensor_reduce(r16[:, :], EQ, AX, ALU.max))
                    if turn == 0:
                        link(dve.tensor_tensor(SEL[:, :, :], EQ, wide(r16), ALU.is_equal))
                        link(dve.scalar_tensor_tensor(out=G2, in0=SEL[:, :, :], scalar=-2.0, in1=G,
                                                      op0=ALU.mult, op1=ALU.add))
                        src = G2
                    else:
                        link(dve.tensor_tensor(EQ, EQ, wide(r16), ALU.is_equal))
                link(dve.tensor_tensor(SEL[:, :, :], SEL[:, :, :], EQ, ALU.add))
                link(dve.tensor_tensor(G2, G, SEL[:, :, :], ALU.mult))

            def ffn0(k):
                layernorm(k)
                gate_top2(k, gb0)
                per_b = G2.rearrange("p (b j) e -> p b j e", b=B)
                link(dve.tensor_tensor(den8, per_b[:, 0], per_b[:, 1], ALU.add))
                link(dve.tensor_scalar(den8, den8, 1e-6, None, ALU.add))
                link(dve.reciprocal(den8, den8))
                for b in range(B):
                    mark(dve.tensor_tensor(RT[:, b].rearrange("p e j -> p j e"), per_b[:, b], den8, ALU.mult))
                settle()
                link(dve.tensor_scalar(RT[:, :, :, :], RT[:, :, :, :], float(B), None, ALU.mult))
                route = RT[:, :, :, :].rearrange("p b e j -> p (b e) j")
                CAv = CA[:, :, :, :].rearrange("p b e j -> p (b e) j")
                CBv = CB[:, :, :, :].rearrange("p b e j -> p (b e) j")
                PTv = PT[:, :, :, :].rearrange("p b e j -> p (b e) j")

                def by_row(t):
                    return t[:, :].unsqueeze(2).to_broadcast([P, NT, J])

                link(dve.memset(thr[:, :], 0.0))
                for r in range(RB):
                    link(dve.tensor_scalar(cand[:, :].bitcast(U32), thr[:, :].bitcast(U32), 1 << (RB - 1 - r), None, ALU.bitwise_or))
                    dve.tensor_tensor(CAv, route, by_row(cand), ALU.is_ge).then_inc(sm(f"cmp{k}"), 1)
                    dve.wait_ge(sm(f"cnt{k}"), r + 1)
                    link(dve.scalar_tensor_tensor(out=took[:, :], in0=bank(3)[:, 0:NT], scalar=KTOP - 0.5, in1=cand[:, :],
                                                  op0=ALU.is_ge, op1=ALU.mult))
                    link(dve.tensor_tensor(thr[:, :], thr[:, :], took[:, :], ALU.max))
                link(dve.scalar_tensor_tensor(out=thr[:, :], in0=thr[:, :], scalar=1.2e-38, in1=thr[:, :],
                                              op0=ALU.is_ge, op1=ALU.mult))
                dve.tensor_tensor(CAv, route, by_row(thr), ALU.is_gt).then_inc(sm(f"gteq{k}"), 1)
                dve.tensor_tensor(CBv, route, by_row(thr), ALU.is_equal).then_inc(sm(f"gteq{k}"), 1)
                dve.wait_ge(sm(f"rank{k}"), 1)
                link(dve.scalar_tensor_tensor(out=PTv, in0=bank(3)[:, 0:NT * J].rearrange("p (n j) -> p n j", j=J),
                                              scalar=KTOP - 0.5, in1=CBv, op0=ALU.is_lt, op1=ALU.mult))
                selv = SEL[:, :, :].rearrange("p (b j) e -> p b e j", b=B)
                for b in range(B):
                    dve.tensor_tensor(selv[:, b], PT[:, b], CA[:, b], ALU.add).then_inc(sm(f"sel{k}"), 1)
                for q in range(NCH):
                    dve.wait_ge(sm(f"t8{k}"), q + 1)
                    dve.tensor_copy(T8B[:, q * CH:(q + 1) * CH], T8[:, q * CH:(q + 1) * CH]).then_inc(sm(f"t8b{k}"), 1)
                n = 0
                for q in range(NCH):
                    for a in range(2):
                        dve.wait_ge(sm(f"spread{k}"), n + 1)
                        dve.wait_ge(sm(f"hid{k}"), n + 1)
                        h = HID[:, a, q * CH:(q + 1) * CH]
                        dve.tensor_tensor(h, h, bank(4 + n % 4), ALU.mult).then_inc(sm(f"hm{k}"), 1)
                        n += 1
                add_back(k, 0.5)

            def add_back(k, scale):
                for q in range(NCH):
                    dve.wait_ge(sm(f"y{k}"), 4 * q + 4)
                    x4 = X[:, 4 * q:4 * q + 4, :].rearrange("p n d -> p (n d)")
                    src = bank(q % 2) if k == 4 else bank(2 + q % 2)
                    dve.scalar_tensor_tensor(out=x4, in0=src, scalar=scale, in1=x4, op0=ALU.mult, op1=ALU.add)\
                        .then_inc(sm(f"xadd{k}"), 1)
                dve.wait_ge(sm(f"xadd{k}"), NCH)

            def ffn1(k):
                layernorm(k)
                gate_top2(k, gb1)
                link(dve.tensor_reduce(r16[:, :], G2, AX, ALU.add))
                link(dve.reciprocal(r16[:, :], r16[:, :]))
                link(dve.tensor_tensor(G2, G2, wide(r16), ALU.mult))
                dve.tensor_scalar(SEL[:, :, :], G2, 0.5, None, ALU.mult).then_inc(sm(f"sel{k}"), 1)
                dve.wait_ge(sm(f"sel{k}"), 1)
                for n in range(NT):
                    dve.wait_ge(sm(f"ye{k}"), n + 1)
                    for e in range(E):
                        y = bank(4 + 2 * (n % 2) + e // 4)[:, (e % 4) * D:(e % 4 + 1) * D]
                        ins = dve.scalar_tensor_tensor(out=X[:, n, :], in0=y, scalar=SEL[:, n, e:e + 1], in1=X[:, n, :],
                                                       op0=ALU.mult, op1=ALU.add)
                        if e < E - 1:
                            link(ins)
                        else:
                            ins.then_inc(sm(f"comb{k}"), 1)
                dve.wait_ge(sm(f"comb{k}"), NT)
                add_back(k, 1.0)

            def split(src, dst, done):
                link(dve.tensor_copy(dst[:, 0, :], src))
                link(dve.tensor_tensor(RES[:, :], src, dst[:, 0, :], ALU.subtract))
                link(dve.tensor_copy(dst[:, 1, :], RES[:, :]))
                dve.tensor_tensor(dst[:, 2, :], RES[:, :], dst[:, 1, :], ALU.subtract).then_inc(sm(done), 1)

            def normalise_batch(b):
                for n in range(b * J, (b + 1) * J):
                    if n >= 2:
                        dve.wait_ge(sm("qktp"), n - 1)
                    for w in range(2):
                        dve.tensor_scalar(QKN[:, n % 2, w, :], RAW[:, n, w, :], mvb[:, n % J, w, 0:1],
                                          rsb[:, n % J, w:w + 1], ALU.subtract, ALU.mult).then_inc(sm("qkn"), 1)
                    if n % 4 == 3:
                        c = n // 4
                        dve.wait_ge(sm("qktp"), n + 1)
                        for w in range(2):
                            dve.tensor_scalar(QF[:, w, :], bank(6 + w), (qsc, ksc)[w][:, 0:1],
                                              (float(DH) ** -0.5, 1.0)[w], ALU.mult, ALU.mult).then_inc(sm("qkt"), 1)
                            dve.wait_ge(sm("qkt"), 2 * c + w + 1)
                        for w in range(2):
                            if c >= 1:
                                dve.wait_ge(sm(f"scr1_{2 * (c - 1) + w}"), 16)
                            split(QF[:, w, :], PARTS[:, w], "parts1")
                            dve.wait_ge(sm("parts1"), 2 * c + w + 1)

            def attention(a, k):
                units = attention_units(a)
                layernorm(k)
                if a == 0:
                    dve.wait_ge(sm("k0_scr"), 16)
                    for c in range(NCH):
                        dve.wait_ge(sm("qf0"), c + 1)
                        if c >= 2:
                            dve.wait_ge(sm(f"scr0_{c - 2}"), 16)
                        split(QF[:, c % 2, :], PARTS[:, c % 2], "parts0")
                        dve.wait_ge(sm("parts0"), c + 1)
                else:
                    for n in range(NT):
                        b, j = n // J, n % J
                        dve.wait_ge(sm("v1"), 2 * (n + 1))
                        for w in range(2):
                            dve.bn_stats(st6b[:, j, w, :], RAW[:, n, w, :]).then_inc(sm("qkst"), 1)
                        if j < J - 1:
                            continue
                        dve.wait_ge(sm("qkst"), 2 * (n + 1))
                        for jj in range(J):
                            for w in range(2):
                                mark(dve.bn_aggr(mvb[:, jj, w, :], st6b[:, jj, w, :]))
                        settle()
                        rsqrt(rsb.rearrange("p n w -> p (n w)"), mvb[:, :, :, 1].rearrange("p n w -> p (n w)"), 1e-6)
                        normalise_batch(b)
                m = 0

                def shift_out(u):
                    nonlocal m
                    dve.wait_ge(sm(f"mxp{a}"), m + 1)
                    if u >= 2:
                        dve.wait_ge(sm(f"mrow{a}_{u % 2}"), 48 * (u // 2))
                    dve.tensor_copy(MT[:, u % 2, :], PS[m % 2][0:12, 0:CH // 2].bitcast(BF16))\
                        .then_inc(sm(f"mxfree{a}"), 1)
                    m += 1

                def finish(b):
                    for par in range(2):
                        dve.wait_ge(sm(f"ogout{a}_{par}"), 128 * 4 * (b + 1))
                    cols = slice(b * S, (b + 1) * S)
                    link(dve.reciprocal(DEN[:, cols], DEN[:, cols]))
                    if a == 0:
                        link(dve.tensor_tensor(NUM[:, cols], NUM[:, cols], DEN[:, cols], ALU.mult))
                        x8 = X[:, b * J:(b + 1) * J, :].rearrange("p n d -> p (n d)")
                        n8 = XN[:, b * J:(b + 1) * J, :].rearrange("p n d -> p (n d)")
                        mark(dve.tensor_tensor(x8, x8, n8, ALU.add))
                        settle()
                        mark(dve.tensor_tensor(x8, x8, NUM[:, cols], ALU.add))
                    else:
                        dve.tensor_tensor(NUM[:, cols], NUM[:, cols], DEN[:, cols], ALU.mult).then_inc(sm("ctx"), 1)

                for u, unit in enumerate(units):
                    for n, (st, i0, nh, w) in enumerate(max_items(unit, a)):
                        if n == 2 and u >= 1:
                            shift_out(u - 1)
                        dve.wait_ge(sm(f"mxp{a}"), m + 1)
                        src = PS[m % 2]
                        if nh == 2:
                            src = src[:, :].rearrange("p (i t) -> p i t", i=2)[:, :, 0:w]
                            dst = MX[:, u % 2, st, i0:i0 + 2]
                        else:
                            src, dst = src[:, 0:w], MX[:, u % 2, st, i0:i0 + 1]
                        dve.tensor_reduce(dst, src, AX, ALU.max).then_inc(sm(f"mxfree{a}"), 1)
                        m += 1
                    dve.wait_ge(sm(f"mxfree{a}"), m)
                    if u >= 2:
                        dve.wait_ge(sm(f"mxfree{a}"), shift_item(a, u - 2) + 1)
                    link(dve.tensor_scalar(MP[:, u % 2, :, 0:4], MX[:, u % 2], -1.0, None, ALU.mult))
                    link(dve.scalar_tensor_tensor(out=MR[:, :, :], in0=MX[:, u % 2], scalar=-1.0, in1=MP[:, u % 2, :, 0:4],
                                                  op0=ALU.mult, op1=ALU.subtract))
                    link(dve.tensor_copy(MP[:, u % 2, :, 4:8], MR[:, :, :]))
                    dve.tensor_tensor(MP[:, u % 2, :, 8:12], MR[:, :, :], MP[:, u % 2, :, 4:8], ALU.subtract)\
                        .then_inc(sm(f"mp{a}"), 1)
                    dve.wait_ge(sm(f"mp{a}"), u + 1)
                shift_out(len(units) - 1)
                for b in range(B):
                    finish(b)
                settle()
                if a == 1:
                    add_back(k, 1.0)

            dve.wait_ge(sm("kf"), 1)
            link(dve.tensor_scalar(QF[:, 0, :], QF[:, 0, :], float(DH) ** -0.5, None, ALU.mult))
            split(QF[:, 0, :], PARTS[:, 0], "k0_parts")
            dve.wait_ge(sm("k0_parts"), 1)
            dve.wait_ge(sm("vp"), 1)
            link(dve.tensor_tensor(RES[:, :].rearrange("p (t d) -> p t d", d=D), bank(4).rearrange("p (t d) -> p t d", d=D),
                                   bvr[:, :].unsqueeze(1).to_broadcast([P, 4, D]), ALU.add))
            for t in range(TK // P):
                mark(dve.tensor_scalar(V0[:, t, :, 0:DH], RES[:, t * D:(t + 1) * D].rearrange("p (h d) -> p h d", h=NH), 0.0,
                                       None, ALU.max))
            settle()
            dve.wait_ge(sm("consts"), N_CONST)
            ffn0(0)
            attention(0, 1)
            ffn0(2)
            ffn1(3)
            attention(1, 4)
            ffn1(5)


_INS = ['L0_attn_queries', 'L0_attn_keys', 'L0_attn_values', 'L0_attn_Wq_w', 'L0_attn_Wq_b', 'L0_attn_Wk_w', 'L0_attn_Wk_b',
        'L0_attn_Wv_w', 'L0_attn_Wv_b', 'L0_ffn_w_gate_w', 'L0_ffn_w_gate_b', 'L0_ffn_W1', 'L0_ffn_b1', 'L0_ffn_W2',
        'L0_ffn_b2', 'L1_attn_W_qkv', 'L1_attn_q_scale', 'L1_attn_k_scale', 'L1_attn_W_out', 'L1_ffn_We', 'L1_ffn_be',
        'L1_ffn_Wg', 'L1_ffn_bg']


def kernel(**inputs):
    import numpy as _np
    import concourse.bacc as _bacc
    from concourse import mybir as _mybir
    from concourse.bass_utils import run_bass_kernel_spmd as _run

    nc = _bacc.Bacc("TRN2", target_bir_lowering=False, num_devices=1)
    arrays, args = {}, {}
    for name in _INS:
        a = _np.ascontiguousarray(inputs[name])
        arrays[f"in_{name}"] = a
        args[name] = nc.dram_tensor(f"in_{name}", a.shape, _mybir.dt.from_np(a.dtype), kind="ExternalInput").ap()
    out = nc.dram_tensor("out_x", (B, S, D), _mybir.dt.float32, kind="ExternalOutput").ap()
    macaron_kernel(nc, args, out)
    r = _run(nc, [arrays], core_ids=[0])
    return r.results[0]["out_x"]
```

```python
from contextlib import ExitStack

import concourse.bass as bass
from concourse import mybir

ALU = mybir.AluOpType
ACT = mybir.ActivationFunctionType
F32 = mybir.dt.float32
BF16 = mybir.dt.bfloat16
U32 = mybir.dt.uint32
I32 = mybir.dt.int32
AX = mybir.AxisListType.X

P = 128
B, S, D = 2, 1024, 128
J = S // P
NT = B * J
E = 8
SUB = 32
KTOP = S // 2
NH, DH = 16, 8
TK = 512
CH = 512
NCH = B * S // CH
RB = 30
SHIFT_ROW = 9 * DH
ROWS = SHIFT_ROW + 3
NSLOT = 8
LEAD = 2
MASKED = -1e30


def attention_units():
    return [(b, c, g) for b in range(B) for c in range(S // CH) for g in range(NH // 4)]


def max_items(unit, causal):
    _, c, _ = unit
    items = []
    for st in range(CH // P):
        if not causal:
            items += [(st, i, 2, TK) for i in (0, 2)]
        elif c == 0:
            items += [(st, i, 2, P * (st + 1)) for i in (0, 2)]
        else:
            items += [(st, i, 1, CH + P * (st + 1)) for i in range(4)]
    return items


def exp_groups(unit, causal):
    _, c, _ = unit
    if not causal:
        return [(tt, 0, False) for tt in range(TK // P)]
    return [(tt, max(0, P * tt - CH * c), P * tt >= CH * c) for tt in range((CH // P) * (c + 1))]


def attention_plan(causal):
    units = attention_units()
    ring, at = [], []
    for u, unit in enumerate(units):
        items = max_items(unit, causal)
        for n, item in enumerate(items):
            if n == 3 and u >= 1:
                at.append(len(ring))
                ring.append(("T", u - 1))
            if n == len(items) - 3 and u in (0, 2, 4) and causal:
                ring.append(("N", u // 2 + 1))
            ring.append(("M", u, item))
        if u in (0, 2, 4):
            ring.append(("Q", u // 2 + 1))
    at.append(len(ring))
    ring.append(("T", len(units) - 1))
    ahead = [min(n + (8 if causal else 6), len(ring)) for n in at] + [len(ring)]
    steps = ring[:ahead[0]]
    done = ahead[0]
    late, finish = None, []
    for u, unit in enumerate(units):
        groups = exp_groups(unit, causal)
        for k, _ in enumerate(groups):
            steps += [("E", u, k, 0), ("E", u, k, 1)]
            upto = ahead[u] + (ahead[u + 1] - ahead[u]) * (2 * k + 1) // (2 * len(groups))
            steps += ring[done:upto]
            done = max(done, upto)
            if late:
                steps.append(("V",) + late)
                if late[0] < u:
                    steps.append(("O", late[0]))
            elif finish and k == 3:
                steps.append(finish.pop())
            if finish and k == 3:
                steps.append(finish.pop())
            late = (u, k)
            steps += [("E", u, k, 2), ("E", u, k, 3)]
            upto = ahead[u] + (ahead[u + 1] - ahead[u]) * (k + 1) // len(groups)
            steps += ring[done:upto]
            done = max(done, upto)
        if u % 4 == 3:
            finish.append(("F",) + unit[:2])
    steps += [("V",) + late, ("O", late[0])] + finish
    assert done == len(ring)
    return steps


def macaron_kernel(nc, A, out):
    ctx = ExitStack()
    with ctx:
        def sb(name, shape, dt=F32):
            return ctx.enter_context(nc.sbuf_tensor(name, shape, dt))

        def sem(name):
            return ctx.enter_context(nc.semaphore(name))

        X = sb("X", [P, NT, D])
        XN = sb("XN", [P, NT, D])
        XT = sb("XT", [P, B * S])
        DEN = sb("DEN", [P, B * S])
        NUM = XT
        QSA = sb("QSA", [P, B * NH * S], BF16)
        QS = QSA[0:ROWS, :].rearrange("p (b h s) -> p b h s", b=B, h=NH)
        RAW = QSA[:, NH * S:2 * NH * S].bitcast(F32)[:, 0:NT * 2 * D].rearrange("p (n w d) -> p n w d", n=NT, w=2)
        KSB = sb("KSB", [P, 2 * NH * S], BF16)
        KS0 = KSB[0:ROWS, NH * TK:2 * NH * TK].rearrange("p (h t) -> p h t", h=NH)
        KS1 = KSB[0:ROWS, :].rearrange("p (b h t) -> p b h t", b=B, h=NH)
        HID = KSB[:, 0:NH * TK].bitcast(F32).rearrange("p (a t) -> p a t", a=2)
        PR = sb("PR", [P, NSLOT, CH])
        V1 = sb("V1", [P, NT, NH, 2 * DH])
        V0 = V1[:, 0:TK // P]
        KF = PR[:, 0, :]
        VF = PR[:, 2, :]
        OG = sb("OG", [P, 2, CH])
        MX = sb("MX", [P, 2, 4, 4])
        MR = sb("MR", [P, 4, 4])
        MP = sb("MP", [P, 2, 4, 12], BF16)
        MT = KSB[96:108, 0:2 * CH].rearrange("p (a c) -> p a c", a=2)
        T8 = DEN[0:E, :]
        T8B = PR[0:E, 6:8, :].rearrange("p a c -> p (a c)").bitcast(BF16)

        ident = sb("ident", [P, P])
        identb = sb("identb", [P, P], BF16)
        onesb = sb("onesb", [P, P], BF16)
        trib = sb("trib", [P, P], BF16)
        maskb = sb("maskb", [P, P], BF16)
        expandb = sb("expandb", [E, 2 * P], BF16)
        prio = sb("prio", [P, E])

        Wg0 = sb("Wg0", [P, E])
        Wg1 = sb("Wg1", [P, E])
        gb0 = sb("gb0", [P, E])
        gb1 = sb("gb1", [P, E])
        W1 = sb("W1", [P, E, SUB])
        b1c = sb("b1c", [P, 2])
        W2 = sb("W2", [P, 2, D])
        b2r = sb("b2r", [E, D])
        We = sb("We", [P, E, D])
        ber = sb("ber", [E, D])
        Wqkv = PR[:, 7, 0:3 * D]
        Wo = sb("Wo", [P, D])
        qsc = sb("qsc", [P, 1])
        ksc = sb("ksc", [P, 1])
        Wraw = XT[:, 0:3 * D].rearrange("p (w d) -> p w d", w=3)
        bvr = XT[:, 3 * D:4 * D]
        PARTS = (DEN[:, 2 * CH:2 * CH + 3 * CH // 2].bitcast(BF16).rearrange("p (q c) -> p q c", q=3),
                 XN[:, :, :].rearrange("p n d -> p (n d)")[:, 2 * CH:2 * CH + 3 * CH // 2].bitcast(BF16)
                 .rearrange("p (q c) -> p q c", q=3))
        QF1 = XN[:, :, :].rearrange("p n d -> p (n d)")[:, 0:2 * CH].rearrange("p (w c) -> p w c", w=2)
        KVraw = XT[:, 2 * CH:4 * CH].rearrange("p (a c) -> p a c", a=2)
        WT = OG[:, 0, 0:3 * D].rearrange("p (w d) -> p w d", w=3)
        bqc = sb("bqc", [P, 1])
        bkc = sb("bkc", [P, 1])
        KVT = DEN[:, 0:2 * TK].rearrange("p (a t) -> p a t", a=2)

        st6 = sb("st6", [P, NT, 6])
        mv = OG[:, 1, 3 * P + 3 * NT:3 * P + 5 * NT].rearrange("p (n c) -> p n c", c=2)
        rstd = OG[:, 1, 3 * P + 5 * NT:3 * P + 6 * NT]
        st6b = OG[:, 0, 0:12 * NT].rearrange("p (n w c) -> p n w c", n=NT, w=2)
        mvb = sb("mvb", [P, NT, 2, 2])
        rsb = sb("rsb", [P, NT, 2])
        RQ = OG[:, 1, 3 * P:3 * P + 3 * NT].rearrange("p (a n) -> p a n", a=3)
        G, G2, GE, EQ = (OG[:, 1, i * NT * E:(i + 1) * NT * E].rearrange("p (n e) -> p n e", e=E) for i in range(4))
        SEL = sb("SEL", [P, NT, E])
        r16 = sb("r16", [P, NT])
        den8 = PR[:, 0, P:P + J * E].rearrange("p (j e) -> p j e", j=J)
        RT = OG[:, 0, 3 * D:4 * D].rearrange("p (b e j) -> p b e j", b=B, e=E)
        PT = PR[:, 0, 0:NT * E].rearrange("p (b e j) -> p b e j", b=B, e=E)
        CA, CB = (PR[:, 1 + i, 0:NT * E // 2].bitcast(BF16).rearrange("p (b e j) -> p b e j", b=B, e=E) for i in range(2))
        thr = sb("thr", [P, NT])
        cand = sb("cand", [P, NT])
        took = sb("took", [P, NT])
        bit = sb("bit", [P, NT], U32)
        steps = sb("steps", [P, 1], I32)

        scrA = nc.dram_tensor("scr_k0", [P, 3, TK], BF16, kind="Internal").ap()
        scrQ0 = nc.dram_tensor("scr_q0", [P, 3, B * S], BF16, kind="Internal").ap()
        scrQ1 = nc.dram_tensor("scr_q1", [P, 3, B * S], BF16, kind="Internal").ap()
        scrK1 = nc.dram_tensor("scr_k1", [P, 3, B * S], BF16, kind="Internal").ap()

        PS = [ctx.enter_context(nc.psum_tensor(f"PS{i}", [P, 2 * CH], F32)) for i in range(4)]

        def bank(i):
            return PS[i // 2][:, (i % 2) * CH:(i % 2 + 1) * CH]

        def expert_bank(n, a):
            return bank((4, 6, 0)[n % 3] + a)

        sems = {}

        def sm(name):
            if name not in sems:
                sems[name] = sem(name)
            return sems[name]

        block = ctx.enter_context(nc.Block())

        PLAN = [attention_plan(False), attention_plan(True)]

        def ring_steps(a):
            return [st for st in PLAN[a] if st[0] in ("M", "T") or (a == 1 and st[0] == "Q")]

        def shift_item(a, u):
            return ring_base(a) + ring_steps(a).index(("T", u))

        def ring_base(a):
            return a

        N_CONST = 4 + 1 + 1 + E + 1

        @block.sync
        def _(sp):
            def load(dst, src, s):
                sp.dma_start(dst, src).then_inc(sm(s), 16)

            for b in range(B):
                load(X[:, b * J:(b + 1) * J, :], A["L0_attn_queries"][b].rearrange("(p j) d -> p j d", j=J), f"x_in{b}")
            load(Wraw[:, 0, :], A["L0_attn_Wq_w"], "kv_in")
            load(Wraw[:, 1, :], A["L0_attn_Wk_w"], "kv_in")
            load(Wraw[:, 2, :], A["L0_attn_Wv_w"], "kv_in")
            load(KVraw[:, 0, :].rearrange("p (t d) -> p t d", d=D), A["L0_attn_keys"][0].rearrange("(t p) d -> p t d", p=P), "kv_in")
            load(KVraw[:, 1, :].rearrange("p (t d) -> p t d", d=D), A["L0_attn_values"][0].rearrange("(t p) d -> p t d", p=P), "kv_in")
            load(bqc[:, :], A["L0_attn_Wq_b"].rearrange("(p o) -> p o", o=1), "kv_in")
            load(bkc[:, :], A["L0_attn_Wk_b"].rearrange("(p o) -> p o", o=1), "kv_in")
            load(bvr[:, :], A["L0_attn_Wv_b"].rearrange("(o d) -> o d", o=1).to_broadcast([P, D]), "kv_in")
            load(Wg0[:, :], A["L0_ffn_w_gate_w"], "f0_in")
            load(gb0[:, :], A["L0_ffn_w_gate_b"].rearrange("(o d) -> o d", o=1).to_broadcast([P, E]), "f0_in")
            load(W1[:, :, :], A["L0_ffn_W1"].rearrange("e d h -> d e h"), "f0_in")
            for a in range(2):
                load(b1c[:, a:a + 1], A["L0_ffn_b1"][4 * a:4 * a + 4].rearrange("e h -> (e h)").rearrange("(p o) -> p o", o=1), "f0_in")
            load(W2[:, :, :], A["L0_ffn_W2"].rearrange("e h d -> (e h) d").rearrange("(a p) d -> p a d", p=P), "f0_in")
            load(b2r[:, :], A["L0_ffn_b2"], "f0_in")
            load(Wg1[:, :], A["L1_ffn_Wg"], "f1_in")
            load(gb1[:, :], A["L1_ffn_bg"].rearrange("(o d) -> o d", o=1).to_broadcast([P, E]), "f1_in")
            load(We[:, :, :], A["L1_ffn_We"].rearrange("e d o -> d e o"), "f1_in")
            load(ber[:, :], A["L1_ffn_be"], "f1_in")
            load(Wo[:, :], A["L1_attn_W_out"], "a1_in")
            load(qsc[:, :], A["L1_attn_q_scale"].rearrange("(p o) -> p o", o=1), "a1_in")
            load(ksc[:, :], A["L1_attn_k_scale"].rearrange("(p o) -> p o", o=1), "a1_in")

            def stack(dst, scr, by_part, s):
                for a in range(3):
                    for c in range(3):
                        r = DH * (3 * a + c)
                        load(dst[r:r + DH], scr.rearrange("(h d) q s -> d q h s", h=NH)[:, a if by_part else c], s)

            def attention_dma(a):
                units = attention_units()
                held = []

                def query_stack(c):
                    b, cols = c // 2, slice((c % 2) * CH, (c % 2 + 1) * CH)
                    here = slice(c * CH, (c + 1) * CH)
                    if a == 0:
                        sp.wait_ge(sm("parts0"), c + 1)
                        load(scrQ0[:, :, here], PARTS[0], f"scr0_{c}")
                        sp.wait_ge(sm(f"scr0_{c}"), 16)
                        stack(QS[:, b, :, cols], scrQ0[:, :, here], True, f"qstack0_{c}")
                        return
                    sp.wait_ge(sm("parts1"), 2 * c + 1)
                    load(scrQ1[:, :, here], PARTS[0], f"scr1_{2 * c}")
                    sp.wait_ge(sm("parts1"), 2 * c + 2)
                    load(scrK1[:, :, here], PARTS[1], f"scr1_{2 * c + 1}")
                    held.append(c)
                    if c == 2:
                        return
                    for h in held:
                        b, cols = h // 2, slice((h % 2) * CH, (h % 2 + 1) * CH)
                        here = slice(h * CH, (h + 1) * CH)
                        sp.wait_ge(sm(f"scr1_{2 * h}"), 16)
                        stack(QS[:, b, :, cols], scrQ1[:, :, here], True, f"qstack1_{h}")
                        sp.wait_ge(sm(f"scr1_{2 * h + 1}"), 16)
                        sp.wait_ge(sm("ks_ones"), 2)
                        stack(KS1[:, b, :, cols], scrK1[:, :, here], False, f"kstack1_{h}")
                    held.clear()

                def shift_rows(u):
                    b, c, g = units[u]
                    sp.wait_ge(sm(f"mxfree{a}"), shift_item(a, u) + 1)
                    for q in range(3):
                        load(QS[SHIFT_ROW + q:SHIFT_ROW + q + 1, b, 4 * g:4 * g + 4, c * CH:(c + 1) * CH],
                             MT[4 * q:4 * q + 4, u % 2, :], f"mrow{a}_{u % 2}")

                def heads_out(u):
                    b, c, g = units[u]
                    sp.wait_ge(sm(f"og{a}"), u + 1)
                    cols = slice(b * S + c * CH, b * S + (c + 1) * CH)
                    for i in range(4):
                        h = 4 * g + i
                        load(NUM[DH * h:DH * h + DH, cols], OG[32 * i:32 * i + DH, u % 2, :], f"ogout{a}_{u % 2}")
                        load(DEN[DH * h:DH * h + DH, cols], OG[32 * i + DH:32 * i + 2 * DH, u % 2, :], f"ogout{a}_{u % 2}")

                query_stack(0)
                for step in PLAN[a]:
                    if step[0] == "Q":
                        query_stack(step[1])
                    elif step[0] == "T":
                        shift_rows(step[1])
                    elif step[0] == "O":
                        heads_out(step[1])

            sp.wait_ge(sm("k0_parts"), 1)
            load(scrA, PARTS[0], "k0_scr")
            sp.wait_ge(sm("k0_scr"), 16)
            sp.wait_ge(sm("ks_ones"), 1)
            stack(KS0, scrA, False, "k0_stack")
            attention_dma(0)
            sp.wait_ge(sm("xadd2"), NCH)
            load(Wqkv, A["L1_attn_W_qkv"], "wqkv_in")
            attention_dma(1)
            for b in range(B):
                sp.wait_ge(sm("xadd5"), NCH // B * (b + 1))
                load(out[b].rearrange("(p j) d -> p j d", j=J), X[:, b * J:(b + 1) * J, :], "stored")
            sp.wait_ge(sm("stored"), 16 * B)

        @block.gpsimd
        def _(pool):
            pool.memset(ident[:, :], 0.0).then_inc(sm("c_set"), 1)
            pool.memset(identb[:, :], 0.0).then_inc(sm("c_set"), 1)
            pool.memset(trib[:, :], 1.0).then_inc(sm("c_set"), 1)
            pool.memset(maskb[:, :], MASKED).then_inc(sm("c_set"), 1)
            pool.memset(expandb[:, :], 1.0).then_inc(sm("c_set"), 1)
            pool.wait_ge(sm("c_set"), 5)
            for m in (ident, identb):
                pool.affine_select(out=m[:, :], in_=m[:, :], compare_op=ALU.not_equal, fill=1.0, base=0,
                                   pattern=[[-1, P]], channel_multiplier=1).then_inc(sm("consts"), 1)
            pool.affine_select(out=trib[:, :], in_=trib[:, :], compare_op=ALU.is_gt, fill=0.0, base=0,
                               pattern=[[1, P]], channel_multiplier=-1).then_inc(sm("consts"), 1)
            pool.affine_select(out=maskb[:, :], in_=maskb[:, :], compare_op=ALU.is_gt, fill=0.0, base=0,
                               pattern=[[1, P]], channel_multiplier=-1).then_inc(sm("consts"), 1)
            pool.affine_select(out=expandb[:, :], in_=expandb[:, :], compare_op=ALU.is_ge, fill=0.0, base=0,
                               pattern=[[1, 2 * P]], channel_multiplier=-SUB).then_inc(sm("c_set"), 1)
            pool.wait_ge(sm("c_set"), 6)
            pool.affine_select(out=expandb[:, :], in_=expandb[:, :], compare_op=ALU.is_ge, fill=0.0, base=SUB - 1,
                               pattern=[[-1, 2 * P]], channel_multiplier=SUB).then_inc(sm("consts"), 1)
            pool.memset(onesb[:, :], 1.0).then_inc(sm("consts"), 1)
            for e in range(E):
                pool.memset(prio[:, e:e + 1], float(E - e)).then_inc(sm("consts"), 1)
            pool.wait_ge(sm("consts"), 4 + 1 + 1 + E)
            pool.memset(KSB[64:96, NH * TK:2 * NH * TK], 1.0).then_inc(sm("ks_ones"), 1)
            pool.wait_ge(sm("ks_ones"), 1)
            pool.memset(V1[:, :, :, DH:2 * DH], 1.0).then_inc(sm("consts"), 1)

            pool.wait_ge(sm("consts"), N_CONST)
            pool.wait_ge(sm("xadd2"), NCH)
            pool.memset(KSB[64:96, :], 1.0).then_inc(sm("ks_ones"), 1)
            pool.wait_ge(sm("ks_ones"), 2)
            n = 0
            for step in PLAN[1]:
                if step[0] != "E":
                    continue
                tt, off, diag = exp_groups(attention_units()[step[1]], True)[step[2]]
                if diag:
                    pool.wait_ge(sm("p1"), n + 1)
                    blk = PR[:, n % NSLOT, off:off + P]
                    pool.affine_select(out=blk, in_=blk, compare_op=ALU.is_ge, fill=0.0, base=0,
                                       pattern=[[1, P]], channel_multiplier=-1).then_inc(sm("pmask"), 1)
                n += 1

        @block.tensor
        def _(pe):
            def transpose_x(k):
                for n in range(NT):
                    q = n // 4
                    pe.wait_ge(sm(f"xn{k}"), n + 1)
                    if q >= 2 and n % 4 == 0:
                        pe.wait_ge(sm(f"xt{k}"), q - 1)
                    pe.transpose(bank(q % 2)[:, (n % 4) * P:(n % 4 + 1) * P], XN[:, n, :], ident[:, :])\
                        .then_inc(sm(f"xtp{k}"), 1)

            def gates(k, Wg):
                for n in range(NT):
                    pe.wait_ge(sm(f"xt{k}"), n // 4 + 1)
                    mm = pe.matmul(bank(2)[:, n * E:(n + 1) * E], XT[:, n * P:(n + 1) * P], Wg[:, :], start=True, stop=True)
                mm.then_inc(sm(f"lg{k}"), 1)

            def transpose_sel(k):
                pe.wait_ge(sm(f"sel{k}"), 2 if k in (0, 2) else 1)
                for n in range(NT):
                    q = n // 4
                    if q >= 2 and n % 4 == 0:
                        pe.wait_ge(sm(f"t8{k}"), q - 1)
                    mm = pe.transpose(bank(2 + q % 2)[0:E, (n % 4) * P:(n % 4 + 1) * P], SEL[:, n, :], ident[:, :])
                    if n % 4 == 3:
                        mm.then_inc(sm(f"t8p{k}"), 1)

            def ffn0(k):
                transpose_x(k)
                pe.wait_ge(sm("f0_in"), 16 * 7)
                gates(k, Wg0)
                n = 0
                for q in range(NCH):
                    for a in range(2):
                        if n >= 4:
                            pe.wait_ge(sm(f"hid{k}"), n - 3)
                        pe.matmul(bank(4 + n % 4), W1[:, 4 * a:4 * a + 4, :].rearrange("p e h -> p (e h)"),
                                  XT[:, q * CH:(q + 1) * CH], start=True, stop=True).then_inc(sm(f"hidp{k}"), 1)
                        n += 1
                def count_tokens():
                    for j in range(J):
                        mm = pe.matmul(bank(3)[:, 0:NT], onesb[:, :], CA[:, :, :, j].rearrange("p b e -> p (b e)"),
                                       start=(j == 0), stop=(j == J - 1))
                    mm.then_inc(sm(f"cnt{k}"), 1)

                pe.wait_ge(sm(f"cmp{k}"), 1)
                count_tokens()
                pe.wait_ge(sm(f"steps{k}"), 1)
                with pe.Fori(0, pe.value_load(steps[0:1, 0:1], min_val=0, max_val=RB)) as r:
                    pe.wait_ge(sm(f"cmp{k}"), r + 2)
                    count_tokens()
                pe.wait_ge(sm(f"gteq{k}"), 2)
                rank = bank(3)[:, 0:NT * J].rearrange("p (n j) -> p n j", j=J)
                for j in range(J):
                    gt = CA[:, :, :, j].rearrange("p b e -> p (b e)").unsqueeze(2).to_broadcast([P, NT, J])
                    eq = CB[:, :, :, j].rearrange("p b e -> p (b e)").unsqueeze(2)
                    pe.matmul(rank, onesb[:, :], gt, start=(j == 0), stop=False)
                    mm = pe.matmul(rank, trib[:, :], eq.to_broadcast([P, NT, J]), start=False, stop=(j == J - 1))
                    if j < J - 1:
                        pe.matmul(rank[:, :, j + 1:J], identb[:, :], eq.to_broadcast([P, NT, J - 1 - j]),
                                  start=False, stop=False)
                mm.then_inc(sm(f"rank{k}"), 1)
                transpose_sel(k)
                n = 0
                for q in range(NCH):
                    pe.wait_ge(sm(f"t8b{k}"), q + 1)
                    for a in range(2):
                        if n >= 4:
                            pe.wait_ge(sm(f"hm{k}"), n - 3)
                        pe.matmul(bank(4 + n % 4), expandb[:, a * P:(a + 1) * P], T8B[:, q * CH:(q + 1) * CH],
                                  start=True, stop=True).then_inc(sm(f"spread{k}"), 1)
                        n += 1
                for n in range(NT):
                    q = n // 4
                    if n % 4 == 0:
                        pe.wait_ge(sm(f"hm{k}"), 2 * q + 2)
                        pe.wait_ge(sm(f"t8{k}"), NCH)
                        if q >= 2:
                            pe.wait_ge(sm(f"xadd{k}"), q - 1)
                    dst = bank(2 + q % 2)[:, (n % 4) * P:(n % 4 + 1) * P]
                    cols = slice(n * P, (n + 1) * P)
                    pe.matmul(dst, HID[:, 0, cols], W2[:, 0, :], start=True, stop=False)
                    pe.matmul(dst, HID[:, 1, cols], W2[:, 1, :], start=False, stop=False)
                    pe.matmul(dst, T8[:, cols], b2r[:, :], start=False, stop=True).then_inc(sm(f"y{k}"), 1)

            def ffn1(k):
                transpose_x(k)
                if k == 3:
                    pe.wait_ge(sm("f1_in"), 16 * 4)
                gates(k, Wg1)
                for n in range(NT):
                    if n >= 3:
                        pe.wait_ge(sm(f"comb{k}"), n - 2)
                    for a in range(2):
                        mm = pe.matmul(expert_bank(n, a), XT[:, n * P:(n + 1) * P],
                                       We[:, 4 * a:4 * a + 4, :].rearrange("p e o -> p (e o)"), start=True, stop=True)
                    mm.then_inc(sm(f"ye{k}"), 1)
                    if n == 2:
                        transpose_sel(k)
                    if n in (4, 5, 8, 12):
                        q = (4, 5, 8, 12).index(n)
                        pe.wait_ge(sm(f"t8{k}"), NCH)
                        if q >= 2:
                            pe.wait_ge(sm(f"xadd{k}"), q - 1)
                        for m in range(4 * q, 4 * q + 4):
                            pe.matmul(bank(2 + q % 2)[:, (m % 4) * P:(m % 4 + 1) * P], T8[:, m * P:(m + 1) * P], ber[:, :],
                                      start=True, stop=True).then_inc(sm(f"y{k}"), 1)

            def keys_values():
                pe.wait_ge(sm("consts"), N_CONST)
                pe.wait_ge(sm("kv_in"), 16 * 8)
                for w in range(3):
                    mm = pe.transpose(bank(0)[:, w * P:(w + 1) * P], Wraw[:, w, :], ident[:, :])
                mm.then_inc(sm("wtp"), 1)
                for a in range(2):
                    for t in range(4):
                        mm = pe.transpose(bank(1 + a)[:, t * P:(t + 1) * P], KVraw[:, a, t * P:(t + 1) * P], ident[:, :])
                    mm.then_inc(sm("wtp"), 1)
                pe.wait_ge(sm("wt"), 2)
                pe.matmul(bank(3), WT[:, 1, :], KVT[:, 0, :], start=True, stop=True).then_inc(sm("kp"), 1)
                pe.wait_ge(sm("wt"), 3)
                for t in range(4):
                    mm = pe.matmul(bank(4)[:, t * P:(t + 1) * P], KVT[:, 1, t * P:(t + 1) * P], WT[:, 2, :],
                                   start=True, stop=True)
                mm.then_inc(sm("vp"), 1)

            def attention(a, k):
                units = attention_units()
                transpose_x(k)
                pe.wait_ge(sm(f"xt{k}"), NCH)
                if a == 0:
                    for c in range(NCH):
                        if c >= 2:
                            pe.wait_ge(sm("qf0"), c - 1)
                        pe.matmul(bank(4 + c % 2), WT[:, 0, :], XT[:, c * CH:(c + 1) * CH], start=True, stop=True)\
                            .then_inc(sm("qp0"), 1)
                    pe.wait_ge(sm("k0_stack"), 16 * 9)
                else:
                    pe.wait_ge(sm("a1_in"), 16 * 3)
                    pe.wait_ge(sm("wqkv_in"), 16)
                    for n in range(NT):
                        if n >= 4:
                            pe.wait_ge(sm("v1"), 2 * (n - 3))
                        pe.matmul(bank(4 + n % 4)[:, 0:3 * D], XT[:, n * P:(n + 1) * P], Wqkv,
                                  start=True, stop=True).then_inc(sm("qkvp"), 1)

                KSof = (lambda b: KS0) if a == 0 else (lambda b: KS1[:, b])
                Vof = (lambda b, tt: V0[:, tt]) if a == 0 else (lambda b, tt: V1[:, b * J + tt])
                m = 0
                n = 0
                pv = 0
                diags = 0

                def ring_tile():
                    if m >= 2:
                        pe.wait_ge(sm(f"mxfree{a}"), m - 1)
                    return PS[m % 2]

                def transpose_qk(c):
                    pe.wait_ge(sm("qkn"), 8 * (c + 1))
                    dst = ring_tile()
                    for t in range(4):
                        for w in range(2):
                            mm = pe.transpose(dst[:, w * CH + t * P:w * CH + (t + 1) * P], RAW[:, 4 * c + t, w, :], ident[:, :])
                    mm.then_inc(sm(f"mxp{a}"), 1)

                if a == 1:
                    transpose_qk(0)
                    m += 1
                stacked = -1
                for step in PLAN[a]:
                    if step[0] == "M":
                        (b, c, g), (st, i0, nh, w) = units[step[1]], step[2]
                        while stacked < 2 * b + c:
                            stacked += 1
                            pe.wait_ge(sm(f"qstack{a}_{stacked}"), 16 * 9)
                            if a == 1:
                                pe.wait_ge(sm(f"kstack1_{stacked}"), 16 * 9)
                        dst = ring_tile()
                        s0 = c * CH + st * P
                        for i in range(i0, i0 + nh):
                            q = QS[0:SHIFT_ROW, b, 4 * g + i, s0:s0 + P]
                            for t0 in range(0, w, CH):
                                t1 = min(w, t0 + CH)
                                o = (i - i0) * CH + t0
                                last = a == 1 and t1 == w
                                mm = pe.matmul(dst[:, o:o + t1 - t0], q, KSof(b)[0:SHIFT_ROW, 4 * g + i, t0:t1],
                                               start=True, stop=not last)
                                if last:
                                    mm = pe.matmul(dst[:, o + t1 - t0 - P:o + t1 - t0], identb[:, :], maskb[:, :],
                                                   start=False, stop=True)
                        mm.then_inc(sm(f"mxp{a}"), 1)
                        m += 1
                    elif step[0] == "T":
                        u = step[1]
                        pe.wait_ge(sm(f"mp{a}"), u + 1)
                        dst = ring_tile()[0:12, 0:CH // 2].bitcast(BF16)
                        for st in range(4):
                            mm = pe.transpose(dst[:, st * P:(st + 1) * P], MP[:, u % 2, st, :], identb[:, :])
                        mm.then_inc(sm(f"mxp{a}"), 1)
                        m += 1
                    elif step[0] == "Q" and a == 1:
                        transpose_qk(step[1])
                        m += 1
                    elif step[0] == "E":
                        _, u, k2, i = step
                        (b, c, g), (tt, off, diag) = units[u], exp_groups(units[u], a)[k2]
                        if k2 == 0 and i == 0:
                            pe.wait_ge(sm(f"mrow{a}_{u % 2}"), 48 * (u // 2 + 1))
                        if n >= 2:
                            pe.wait_ge(sm(f"p{a}"), n - 1)
                        elif a == 0:
                            pe.wait_ge(sm("qf0"), NCH)
                        else:
                            pe.wait_ge(sm("v1"), 2 * NT)
                        pe.matmul(bank(4 + n % 2)[:, 0:CH - off], KSof(b)[0:ROWS, 4 * g + i, tt * P:(tt + 1) * P],
                                  QS[0:ROWS, b, 4 * g + i, c * CH + off:(c + 1) * CH], start=True, stop=True)\
                            .then_inc(sm(f"sc{a}"), 1)
                        n += 1
                    elif step[0] == "V":
                        _, u, k2 = step
                        groups = exp_groups(units[u], a)
                        (b, c, g), (tt, off, diag) = units[u], groups[k2]
                        if k2 == 0 and u >= 2:
                            pe.wait_ge(sm(f"og{a}"), u - 1)
                        if a == 1 and diag:
                            diags += 4
                            pe.wait_ge(sm("pmask"), diags)
                        pe.wait_ge(sm(f"p{a}"), pv + 4)
                        for i in range(4):
                            pe.matmul(bank(6 + u % 2)[32 * i:32 * i + 2 * DH, off:CH], Vof(b, tt)[:, 4 * g + i, :],
                                      PR[:, pv % NSLOT, off:CH], start=k2 == 0, stop=k2 == len(groups) - 1)\
                                .then_inc(sm(f"pv{a}"), 1)
                            pv += 1
                if a == 1:
                    for n in range(NT):
                        q = n // 4
                        if n % 4 == 0:
                            pe.wait_ge(sm("ctx"), 2 * (q // 2) + 2)
                            if q >= 2:
                                pe.wait_ge(sm(f"xadd{k}"), q - 1)
                        b, j = n // J, n % J
                        pe.matmul(bank(q % 2)[:, (n % 4) * P:(n % 4 + 1) * P],
                                  NUM[:, b * S:(b + 1) * S].rearrange("p (s j) -> p j s", j=J)[:, j, :], Wo[:, :],
                                  start=True, stop=True).then_inc(sm(f"y{k}"), 1)

            keys_values()
            ffn0(0)
            attention(0, 1)
            ffn0(2)
            ffn1(3)
            attention(1, 4)
            ffn1(5)

        @block.scalar
        def _(act):
            def copy_xt(k, natural):
                for q in range(NCH):
                    act.wait_ge(sm(f"xtp{k}"), 4 * q + 4)
                    if natural:
                        b, j0 = q // 2, 4 * (q % 2)
                        dst = XT[:, b * S:(b + 1) * S].rearrange("d (p j) -> d j p", j=J)[:, j0:j0 + 4, :]
                        src = bank(q % 2).rearrange("d (j p) -> d j p", p=P)
                    else:
                        dst, src = XT[:, q * CH:(q + 1) * CH], bank(q % 2)
                    act.activation(dst, src, ACT.Copy).then_inc(sm(f"xt{k}"), 1)

            def gate_exp(k):
                act.wait_ge(sm(f"gsub{k}"), 1)
                act.activation(GE, G, ACT.Exp).then_inc(sm(f"gexp{k}"), 1)

            def copy_t8(k):
                if k == 0:
                    act.wait_ge(sm("k0_scr"), 16)
                for q in range(NCH):
                    act.wait_ge(sm(f"t8p{k}"), q + 1)
                    act.activation(T8[:, q * CH:(q + 1) * CH], bank(2 + q % 2)[0:E, :], ACT.Copy).then_inc(sm(f"t8{k}"), 1)

            def ffn0(k):
                copy_xt(k, False)
                gate_exp(k)
                n = 0
                for q in range(NCH):
                    for a in range(2):
                        act.wait_ge(sm(f"hidp{k}"), n + 1)
                        act.activation(HID[:, a, q * CH:(q + 1) * CH], bank(4 + n % 4), ACT.Gelu, bias=b1c[:, a:a + 1])\
                            .then_inc(sm(f"hid{k}"), 1)
                        n += 1
                copy_t8(k)

            def ffn1(k):
                copy_xt(k, False)
                gate_exp(k)
                copy_t8(k)

            def attention(a, k):
                units = attention_units()
                copy_xt(k, True)
                if a == 0:
                    for c in range(NCH):
                        act.wait_ge(sm("qp0"), c + 1)
                        act.activation(XT[:, c * CH:(c + 1) * CH], bank(4 + c % 2), ACT.Relu, bias=bqc[:, 0:1]).then_inc(sm("qf0"), 1)
                else:
                    for n in range(NT):
                        act.wait_ge(sm("qkvp"), n + 1)
                        act.activation(RAW[:, n], bank(4 + n % 4)[:, 0:2 * D].rearrange("p (w d) -> p w d", w=2), ACT.Copy)\
                            .then_inc(sm("v1"), 1)
                        act.activation(V1[:, n, :, 0:DH], bank(4 + n % 4)[:, 2 * D:3 * D].rearrange("p (h d) -> p h d", h=NH),
                                       ACT.Copy).then_inc(sm("v1"), 1)
                n = 0
                sums = 0
                for step in PLAN[a]:
                    if step[0] == "E":
                        off = exp_groups(units[step[1]], a)[step[2]][1]
                        act.wait_ge(sm(f"sc{a}"), n + 1)
                        if n >= NSLOT:
                            act.wait_ge(sm(f"pv{a}"), n - NSLOT + 1)
                        act.activation(PR[:, n % NSLOT, off:CH], bank(4 + n % 2)[:, 0:CH - off], ACT.Exp)\
                            .then_inc(sm(f"p{a}"), 1)
                        n += 1
                    elif step[0] == "O":
                        u = step[1]
                        sums += 4 * len(exp_groups(units[u], a))
                        act.wait_ge(sm(f"pv{a}"), sums)
                        if u >= 2:
                            act.wait_ge(sm(f"ogout{a}_{u % 2}"), 128 * (u // 2))
                        act.activation(OG[:, u % 2, :], bank(6 + u % 2), ACT.Copy).then_inc(sm(f"og{a}"), 1)

            act.wait_ge(sm("wtp"), 1)
            act.activation(WT[:, :, :].rearrange("p w d -> p (w d)"), bank(0)[:, 0:3 * P], ACT.Copy).then_inc(sm("wt"), 1)
            for a in range(2):
                act.wait_ge(sm("wtp"), 2 + a)
                act.activation(KVT[:, a, :], bank(1 + a), ACT.Copy).then_inc(sm("wt"), 1)
            act.wait_ge(sm("kp"), 1)
            act.activation(KF, bank(3), ACT.Relu, bias=bkc[:, 0:1]).then_inc(sm("kf"), 1)
            ffn0(0)
            attention(0, 1)
            ffn0(2)
            ffn1(3)
            attention(1, 4)
            ffn1(5)

        @block.vector
        def _(dve):
            chain = [0]

            def link(ins):
                chain[0] += 1
                ins.then_inc(sm("dve_chain"), 1)
                dve.wait_ge(sm("dve_chain"), chain[0])

            def mark(ins):
                chain[0] += 1
                ins.then_inc(sm("dve_chain"), 1)

            def settle():
                dve.wait_ge(sm("dve_chain"), chain[0])

            def rsqrt(dst, src, eps):
                a, y, t = RQ[:, 0, :], RQ[:, 1, :], RQ[:, 2, :]
                link(dve.tensor_scalar(a, src, eps, None, ALU.add))
                link(dve.tensor_scalar(t.bitcast(I32), a.bitcast(I32), 1, None, ALU.logical_shift_right))
                link(dve.tensor_scalar(y.bitcast(I32), t.bitcast(I32), -1.0, float(0x5f3759df), ALU.mult, ALU.add))
                for step in range(3):
                    link(dve.scalar_tensor_tensor(out=t, in0=y, scalar=-0.5, in1=y, op0=ALU.mult, op1=ALU.mult))
                    link(dve.tensor_tensor(t, t, a, ALU.mult))
                    link(dve.scalar_tensor_tensor(out=(dst if step == 2 else y), in0=t, scalar=1.5, in1=y,
                                                  op0=ALU.add, op1=ALU.mult))

            def layernorm(k):
                settle()
                for n in range(NT):
                    if k == 0 and n % J == 0:
                        dve.wait_ge(sm(f"x_in{n // J}"), 16)
                    mark(dve.bn_stats(st6[:, n, :], X[:, n, :]))
                settle()
                for n in range(NT):
                    mark(dve.bn_aggr(mv[:, n, :], st6[:, n, :]))
                settle()
                rsqrt(rstd[:, :], mv[:, :, 1], 1e-5)
                for n in range(NT):
                    dve.tensor_scalar(XN[:, n, :], X[:, n, :], mv[:, n, 0:1], rstd[:, n:n + 1], ALU.subtract, ALU.mult)\
                        .then_inc(sm(f"xn{k}"), 1)
                dve.wait_ge(sm(f"xn{k}"), NT)

            def wide(t):
                return t[:, :].unsqueeze(2).to_broadcast([P, NT, E])

            def gate_top2(k, gb):
                pri = prio[:, :].unsqueeze(1).to_broadcast([P, NT, E])
                logits = bank(2)[:, 0:NT * E].rearrange("p (n e) -> p n e", e=E)
                dve.wait_ge(sm(f"lg{k}"), 1)
                link(dve.tensor_tensor(G, logits, gb[:, :].unsqueeze(1).to_broadcast([P, NT, E]), ALU.add))
                link(dve.tensor_reduce(r16[:, :], G, AX, ALU.max))
                dve.tensor_tensor(G, G, wide(r16), ALU.subtract).then_inc(sm(f"gsub{k}"), 1)
                dve.wait_ge(sm(f"gexp{k}"), 1)
                link(dve.tensor_reduce(r16[:, :], GE, AX, ALU.add))
                link(dve.reciprocal(r16[:, :], r16[:, :]))
                link(dve.tensor_tensor(G, GE, wide(r16), ALU.mult))
                src = G
                for turn in range(2):
                    link(dve.tensor_reduce(r16[:, :], src[:, :, :], AX, ALU.max))
                    link(dve.tensor_tensor(EQ, src[:, :, :], wide(r16), ALU.is_equal))
                    link(dve.tensor_tensor(EQ, EQ, pri, ALU.mult))
                    link(dve.tensor_reduce(r16[:, :], EQ, AX, ALU.max))
                    if turn == 0:
                        link(dve.tensor_tensor(SEL[:, :, :], EQ, wide(r16), ALU.is_equal))
                        link(dve.scalar_tensor_tensor(out=G2, in0=SEL[:, :, :], scalar=-2.0, in1=G,
                                                      op0=ALU.mult, op1=ALU.add))
                        src = G2
                    else:
                        link(dve.tensor_tensor(EQ, EQ, wide(r16), ALU.is_equal))
                link(dve.tensor_tensor(SEL[:, :, :], SEL[:, :, :], EQ, ALU.add))
                link(dve.tensor_tensor(G2, G, SEL[:, :, :], ALU.mult))

            def ffn0(k):
                layernorm(k)
                gate_top2(k, gb0)
                per_b = G2.rearrange("p (b j) e -> p b j e", b=B)
                link(dve.tensor_tensor(den8, per_b[:, 0], per_b[:, 1], ALU.add))
                link(dve.tensor_scalar(den8, den8, 1e-6, None, ALU.add))
                link(dve.reciprocal(den8, den8))
                for b in range(B):
                    mark(dve.tensor_tensor(RT[:, b].rearrange("p e j -> p j e"), per_b[:, b], den8, ALU.mult))
                settle()
                link(dve.tensor_scalar(RT[:, :, :, :], RT[:, :, :, :], float(B), None, ALU.mult))
                route = RT[:, :, :, :].rearrange("p b e j -> p (b e) j")
                CAv = CA[:, :, :, :].rearrange("p b e j -> p (b e) j")
                CBv = CB[:, :, :, :].rearrange("p b e j -> p (b e) j")
                PTv = PT[:, :, :, :].rearrange("p b e j -> p (b e) j")

                def by_row(t):
                    return t[:, :].unsqueeze(2).to_broadcast([P, NT, J])

                dve.tensor_scalar(CAv, route, 0.0, None, ALU.is_gt).then_inc(sm(f"cmp{k}"), 1)
                mark(dve.memset(thr[:, :], 0.0))
                link(dve.memset(bit[:, :], 1 << (RB - 1)))
                dve.wait_ge(sm(f"cnt{k}"), 1)
                link(dve.tensor_reduce(took[:, 0:1], bank(3)[:, 0:NT], AX, ALU.max))
                dve.tensor_scalar(steps[:, :], took[:, 0:1], KTOP + 0.5, float(RB), ALU.is_ge, ALU.mult).then_inc(sm(f"steps{k}"), 1)
                dve.wait_ge(sm(f"steps{k}"), 1)
                with dve.Fori(0, dve.value_load(steps[0:1, 0:1], min_val=0, max_val=RB)) as r:
                    dve.tensor_tensor(cand[:, :].bitcast(U32), thr[:, :].bitcast(U32), bit[:, :], ALU.bitwise_or)\
                        .then_inc(sm(f"cand{k}"), 1)
                    dve.wait_ge(sm(f"cand{k}"), r + 1)
                    dve.tensor_tensor(CAv, route, by_row(cand), ALU.is_ge).then_inc(sm(f"cmp{k}"), 1)
                    dve.wait_ge(sm(f"cnt{k}"), r + 2)
                    dve.scalar_tensor_tensor(out=took[:, :], in0=bank(3)[:, 0:NT], scalar=KTOP - 0.5, in1=cand[:, :],
                                             op0=ALU.is_ge, op1=ALU.mult).then_inc(sm(f"took{k}"), 1)
                    dve.wait_ge(sm(f"took{k}"), r + 1)
                    dve.tensor_scalar(bit[:, :], bit[:, :], 1, None, ALU.logical_shift_right).then_inc(sm(f"thr{k}"), 1)
                    dve.tensor_tensor(thr[:, :], thr[:, :], took[:, :], ALU.max).then_inc(sm(f"thr{k}"), 1)
                    dve.wait_ge(sm(f"thr{k}"), r * 2 + 2)
                link(dve.scalar_tensor_tensor(out=thr[:, :], in0=thr[:, :], scalar=1.2e-38, in1=thr[:, :],
                                              op0=ALU.is_ge, op1=ALU.mult))
                dve.tensor_tensor(CAv, route, by_row(thr), ALU.is_gt).then_inc(sm(f"gteq{k}"), 1)
                dve.tensor_tensor(CBv, route, by_row(thr), ALU.is_equal).then_inc(sm(f"gteq{k}"), 1)
                dve.wait_ge(sm(f"rank{k}"), 1)
                link(dve.scalar_tensor_tensor(out=PTv, in0=bank(3)[:, 0:NT * J].rearrange("p (n j) -> p n j", j=J),
                                              scalar=KTOP - 0.5, in1=CBv, op0=ALU.is_lt, op1=ALU.mult))
                selv = SEL[:, :, :].rearrange("p (b j) e -> p b e j", b=B)
                for b in range(B):
                    dve.tensor_tensor(selv[:, b], PT[:, b], CA[:, b], ALU.add).then_inc(sm(f"sel{k}"), 1)
                for q in range(NCH):
                    dve.wait_ge(sm(f"t8{k}"), q + 1)
                    dve.tensor_copy(T8B[:, q * CH:(q + 1) * CH], T8[:, q * CH:(q + 1) * CH]).then_inc(sm(f"t8b{k}"), 1)
                n = 0
                for q in range(NCH):
                    for a in range(2):
                        dve.wait_ge(sm(f"spread{k}"), n + 1)
                        dve.wait_ge(sm(f"hid{k}"), n + 1)
                        h = HID[:, a, q * CH:(q + 1) * CH]
                        dve.tensor_tensor(h, h, bank(4 + n % 4), ALU.mult).then_inc(sm(f"hm{k}"), 1)
                        n += 1
                add_back(k, 0.5)

            def add_chunk(k, scale, q):
                dve.wait_ge(sm(f"y{k}"), 4 * q + 4)
                if k in (3, 5):
                    dve.wait_ge(sm(f"comb{k}"), 4 * q + 4)
                x4 = X[:, 4 * q:4 * q + 4, :].rearrange("p n d -> p (n d)")
                src = bank(q % 2) if k == 4 else bank(2 + q % 2)
                dve.scalar_tensor_tensor(out=x4, in0=src, scalar=scale, in1=x4, op0=ALU.mult, op1=ALU.add)\
                    .then_inc(sm(f"xadd{k}"), 1)

            def add_back(k, scale):
                for q in range(NCH):
                    add_chunk(k, scale, q)
                dve.wait_ge(sm(f"xadd{k}"), NCH)

            def ffn1(k):
                layernorm(k)
                gate_top2(k, gb1)
                link(dve.tensor_reduce(r16[:, :], G2, AX, ALU.add))
                link(dve.reciprocal(r16[:, :], r16[:, :]))
                link(dve.tensor_tensor(G2, G2, wide(r16), ALU.mult))
                dve.tensor_scalar(SEL[:, :, :], G2, 0.5, None, ALU.mult).then_inc(sm(f"sel{k}"), 1)
                dve.wait_ge(sm(f"sel{k}"), 1)
                ops = sorted((4 * n + e, n, e) for n in range(NT) for e in range(E))
                added = {}
                for _, n, e in ops:
                    if e == 0:
                        dve.wait_ge(sm(f"ye{k}"), n + 1)
                    else:
                        dve.wait_ge(sm("dve_chain"), added[n])
                    ins = dve.scalar_tensor_tensor(out=X[:, n, :], in0=expert_bank(n, e // 4)[:, (e % 4) * D:(e % 4 + 1) * D],
                                                   scalar=SEL[:, n, e:e + 1], in1=X[:, n, :], op0=ALU.mult, op1=ALU.add)
                    if e < E - 1:
                        mark(ins)
                        added[n] = chain[0]
                    else:
                        ins.then_inc(sm(f"comb{k}"), 1)
                        if n % 4 == 1 and n > 4:
                            add_chunk(k, 1.0, n // 4 - 1)
                add_chunk(k, 1.0, NCH - 1)
                dve.wait_ge(sm(f"xadd{k}"), NCH)

            def split(src, dst, done):
                link(dve.tensor_copy(dst[:, 0, :], src))
                link(dve.tensor_tensor(src, src, dst[:, 0, :], ALU.subtract))
                link(dve.tensor_copy(dst[:, 1, :], src))
                dve.tensor_tensor(dst[:, 2, :], src, dst[:, 1, :], ALU.subtract).then_inc(sm(done), 1)

            def attention(a, k):
                units = attention_units()
                layernorm(k)
                m = 0

                def prepare(c):
                    nonlocal m
                    if a == 0:
                        dve.wait_ge(sm("qf0"), c + 1)
                        if c >= 1:
                            dve.wait_ge(sm(f"scr0_{c - 1}"), 16)
                        split(XT[:, c * CH:(c + 1) * CH], PARTS[0], "parts0")
                        dve.wait_ge(sm("parts0"), c + 1)
                        return
                    dve.wait_ge(sm(f"mxp{a}"), m + 1)
                    for w in range(2):
                        ins = dve.tensor_scalar(QF1[:, w, :], PS[m % 2][:, w * CH:(w + 1) * CH], (qsc, ksc)[w][:, 0:1],
                                                (float(DH) ** -0.5, 1.0)[w], ALU.mult, ALU.mult)
                        if w == 0:
                            mark(ins)
                    ins.then_inc(sm(f"mxfree{a}"), 1)
                    settle()
                    m += 1
                    dve.wait_ge(sm(f"mxfree{a}"), m)
                    for w in range(2):
                        if c >= 1:
                            dve.wait_ge(sm(f"scr1_{2 * (c - 1) + w}"), 16)
                        split(QF1[:, w, :], PARTS[w], "parts1")
                    dve.wait_ge(sm("parts1"), 2 * c + 2)

                def normalise(c):
                    for n in range(4 * c, 4 * c + 4):
                        for w in range(2):
                            dve.tensor_scalar(RAW[:, n, w, :], RAW[:, n, w, :], mvb[:, n, w, 0:1], rsb[:, n, w:w + 1],
                                              ALU.subtract, ALU.mult).then_inc(sm("qkn"), 1)

                def statistics(b):
                    for n in range(b * J, (b + 1) * J):
                        dve.wait_ge(sm("v1"), 2 * n + 1)
                        for w in range(2):
                            mark(dve.bn_stats(st6b[:, n, w, :], RAW[:, n, w, :]))
                    settle()
                    for n in range(b * J, (b + 1) * J):
                        for w in range(2):
                            mark(dve.bn_aggr(mvb[:, n, w, :], st6b[:, n, w, :]))
                    settle()
                    rsqrt(rsb[:, b * J:(b + 1) * J, :].rearrange("p n w -> p (n w)"),
                          mvb[:, b * J:(b + 1) * J, :, 1].rearrange("p n w -> p (n w)"), 1e-6)

                if a == 1:
                    statistics(0)
                    normalise(0)
                    prepare(0)
                    statistics(1)
                else:
                    prepare(0)
                for at, step in enumerate(PLAN[a]):
                    if step[0] == "M":
                        _, u, (st, i0, nh, w) = step
                        dve.wait_ge(sm(f"mxp{a}"), m + 1)
                        src = PS[m % 2]
                        if nh == 2:
                            src = src[:, :].rearrange("p (i t) -> p i t", i=2)[:, :, 0:w]
                            dst = MX[:, u % 2, st, i0:i0 + 2]
                        else:
                            src, dst = src[:, 0:w], MX[:, u % 2, st, i0:i0 + 1]
                        dve.tensor_reduce(dst, src, AX, ALU.max).then_inc(sm(f"mxfree{a}"), 1)
                        m += 1
                        if step[2] != max_items(units[u], a)[-1]:
                            continue
                        dve.wait_ge(sm(f"mxfree{a}"), m)
                        if u >= 2:
                            dve.wait_ge(sm(f"mxfree{a}"), shift_item(a, u - 2) + 1)
                        link(dve.tensor_scalar(MP[:, u % 2, :, 0:4], MX[:, u % 2], -1.0, None, ALU.mult))
                        link(dve.scalar_tensor_tensor(out=MR[:, :, :], in0=MX[:, u % 2], scalar=-1.0, in1=MP[:, u % 2, :, 0:4],
                                                      op0=ALU.mult, op1=ALU.subtract))
                        link(dve.tensor_copy(MP[:, u % 2, :, 4:8], MR[:, :, :]))
                        dve.tensor_tensor(MP[:, u % 2, :, 8:12], MR[:, :, :], MP[:, u % 2, :, 4:8], ALU.subtract)\
                            .then_inc(sm(f"mp{a}"), 1)
                        dve.wait_ge(sm(f"mp{a}"), u + 1)
                    elif step[0] == "T":
                        u = step[1]
                        dve.wait_ge(sm(f"mxp{a}"), m + 1)
                        if u >= 2:
                            dve.wait_ge(sm(f"mrow{a}_{u % 2}"), 48 * (u // 2))
                        dve.tensor_copy(MT[:, u % 2, :], PS[m % 2][0:12, 0:CH // 2].bitcast(BF16))\
                            .then_inc(sm(f"mxfree{a}"), 1)
                        m += 1
                    elif step[0] == "N":
                        normalise(step[1])
                    elif step[0] == "Q":
                        prepare(step[1])
                    elif step[0] == "F":
                        _, b, c = step
                        for par in range(2):
                            dve.wait_ge(sm(f"ogout{a}_{par}"), 128 * 2 * (2 * b + c + 1))
                        cols = slice(b * S + c * CH, b * S + (c + 1) * CH)
                        link(dve.reciprocal(DEN[:, cols], DEN[:, cols]))
                        if a == 0:
                            link(dve.tensor_tensor(NUM[:, cols], NUM[:, cols], DEN[:, cols], ALU.mult))
                            x4 = X[:, :, :].rearrange("p n d -> p (n d)")[:, cols]
                            n4 = XN[:, :, :].rearrange("p n d -> p (n d)")[:, cols]
                            link(dve.tensor_tensor(x4, x4, n4, ALU.add))
                            link(dve.tensor_tensor(x4, x4, NUM[:, cols], ALU.add))
                        else:
                            dve.tensor_tensor(NUM[:, cols], NUM[:, cols], DEN[:, cols], ALU.mult).then_inc(sm("ctx"), 1)
                settle()
                if a == 1:
                    add_back(k, 1.0)

            dve.wait_ge(sm("kf"), 1)
            link(dve.tensor_scalar(KF, KF, float(DH) ** -0.5, None, ALU.mult))
            split(KF, PARTS[0], "k0_parts")
            dve.wait_ge(sm("k0_parts"), 1)
            dve.wait_ge(sm("vp"), 1)
            link(dve.tensor_tensor(VF.rearrange("p (t d) -> p t d", d=D), bank(4).rearrange("p (t d) -> p t d", d=D),
                                   bvr[:, :].unsqueeze(1).to_broadcast([P, 4, D]), ALU.add))
            for t in range(TK // P):
                mark(dve.tensor_scalar(V0[:, t, :, 0:DH], VF[:, t * D:(t + 1) * D].rearrange("p (h d) -> p h d", h=NH), 0.0,
                                       None, ALU.max))
            settle()
            dve.wait_ge(sm("consts"), N_CONST)
            ffn0(0)
            attention(0, 1)
            ffn0(2)
            ffn1(3)
            attention(1, 4)
            ffn1(5)


_INS = ['L0_attn_queries', 'L0_attn_keys', 'L0_attn_values', 'L0_attn_Wq_w', 'L0_attn_Wq_b', 'L0_attn_Wk_w', 'L0_attn_Wk_b',
        'L0_attn_Wv_w', 'L0_attn_Wv_b', 'L0_ffn_w_gate_w', 'L0_ffn_w_gate_b', 'L0_ffn_W1', 'L0_ffn_b1', 'L0_ffn_W2',
        'L0_ffn_b2', 'L1_attn_W_qkv', 'L1_attn_q_scale', 'L1_attn_k_scale', 'L1_attn_W_out', 'L1_ffn_We', 'L1_ffn_be',
        'L1_ffn_Wg', 'L1_ffn_bg']


def kernel(**inputs):
    import numpy as _np
    import concourse.bacc as _bacc
    from concourse import mybir as _mybir
    from concourse.bass_utils import run_bass_kernel_spmd as _run

    nc = _bacc.Bacc("TRN2", target_bir_lowering=False, num_devices=1)
    arrays, args = {}, {}
    for name in _INS:
        a = _np.ascontiguousarray(inputs[name])
        arrays[f"in_{name}"] = a
        args[name] = nc.dram_tensor(f"in_{name}", a.shape, _mybir.dt.from_np(a.dtype), kind="ExternalInput").ap()
    out = nc.dram_tensor("out_x", (B, S, D), _mybir.dt.float32, kind="ExternalOutput").ap()
    macaron_kernel(nc, args, out)
    r = _run(nc, [arrays], core_ids=[0])
    return r.results[0]["out_x"]
```

```python
from contextlib import ExitStack

import concourse.bass as bass
from concourse import mybir

ALU = mybir.AluOpType
ACT = mybir.ActivationFunctionType
F32 = mybir.dt.float32
BF16 = mybir.dt.bfloat16
U32 = mybir.dt.uint32
I32 = mybir.dt.int32
AX = mybir.AxisListType.X

P = 128
B, S, D = 2, 1024, 128
J = S // P
NT = B * J
E = 8
SUB = 32
KTOP = S // 2
NH, DH = 16, 8
TK = 512
CH = 512
NCH = B * S // CH
RB = 30
SHIFT_ROW = 9 * DH
ROWS = SHIFT_ROW + 3
NSLOT = 8
AHEAD_L0, AHEAD_L1 = 8, 20
STACK_BEHIND = ({0: ((1, 0),), 1: ((1, 1),), 2: ((1, 2), (2, 0)), 3: ((2, 1),), 4: ((2, 2), (3, 0)), 5: ((3, 1),), 6: ((3, 2),)},
                {1: ((1, 0), (1, 1), (1, 2)), 5: ((2, 0), (2, 1)), 6: ((2, 2),), 7: ((3, 0),), 8: ((3, 1),), 9: ((3, 2),)})
SHIFT_LEAD = 6
FP = 4
MASKED = -1e30


def attention_units():
    return [(b, c, g) for b in range(B) for c in range(S // CH) for g in range(NH // 4)]


def max_items(unit, causal):
    _, c, _ = unit
    items = []
    for st in range(CH // P):
        if not causal or c == 1:
            items += [(st, 0, CH, i, 1) for i in range(4)]
        if causal:
            w = P * (st + 1)
            nh = {1: 4, 2: 2, 3: 1, 4: 1}[st + 1]
            items += [(st, c * CH, w, i, nh) for i in range(0, 4, nh)]
    return items


def exp_groups(unit, causal):
    _, c, _ = unit
    if not causal:
        return [(tt, 0, False) for tt in range(TK // P)]
    return [(tt, max(0, P * tt - CH * c), P * tt >= CH * c) for tt in range((CH // P) * (c + 1))]


def attention_plan(causal):
    units = attention_units()
    ring, at = [], []
    for u, unit in enumerate(units):
        items = max_items(unit, causal)
        for n, item in enumerate(items):
            if n == 6 and u >= 1:
                at.append(len(ring))
                ring.append(("T", u - 1))
            if causal and u in (0, 2, 4) and len(items) - 9 <= n < len(items) - 1:
                ring.append(("N", u // 2 + 1, n - (len(items) - 9)))
            if causal and u in (1, 3, 5) and n < 8:
                ring.append(("R", u // 2 + 1, n))
            ring.append(("M", u, item))
        if u in (0, 2, 4):
            ring.append(("Q", u // 2 + 1))
    at.append(len(ring))
    ring.append(("T", len(units) - 1))
    ahead = [min(n + (AHEAD_L1 if causal else AHEAD_L0), len(ring)) for n in at] + [len(ring)]
    steps = ring[:ahead[0]]
    done = ahead[0]
    late, finish = None, []

    def between():
        if late:
            steps.append(("V",) + late)
            if late[0] < u:
                steps.append(("O", late[0]))
        if finish and k >= 2:
            steps.append(finish.pop(0))

    for u, unit in enumerate(units):
        groups = exp_groups(unit, causal)
        for k, _ in enumerate(groups):
            for i in range(4):
                if i == (3 if causal else 2):
                    between()
                    if causal and u == len(units) - 1 and k == 4:
                        steps.append(("Y",))
                steps.append(("E", u, k, i))
                span = 4 * len(groups) - (SHIFT_LEAD if u == len(units) - 2 else 0)
                upto = ahead[u] + (ahead[u + 1] - ahead[u]) * min(span, 4 * k + i + 1) // span
                steps += ring[done:upto]
                done = max(done, upto)
            late = (u, k)
        if u % 4 == 3:
            finish += [("F",) + unit[:2] + (i,) for i in range(FP)]
    steps += [("V",) + late, ("O", late[0])] + finish
    assert done == len(ring)
    return steps


def macaron_kernel(nc, A, out):
    ctx = ExitStack()
    with ctx:
        def sb(name, shape, dt=F32):
            return ctx.enter_context(nc.sbuf_tensor(name, shape, dt))

        def sem(name):
            return ctx.enter_context(nc.semaphore(name))

        X = sb("X", [P, NT, D])
        XN = sb("XN", [P, NT, D])
        XD = sb("XD", [P, 2, B * S])
        XT = XD[:, 0, :]
        DEN = XD[:, 1, :]
        NUM = XT
        QSA = sb("QSA", [P, B * NH * S], BF16)
        QS = QSA[0:ROWS, :].rearrange("p (b h s) -> p b h s", b=B, h=NH)
        RAW = QSA[:, NH * S:2 * NH * S].bitcast(F32)[:, 0:NT * 2 * D].rearrange("p (n w d) -> p n w d", n=NT, w=2)
        KSB = sb("KSB", [P, 2 * NH * S], BF16)
        KS0 = KSB[0:ROWS, NH * TK:2 * NH * TK].rearrange("p (h t) -> p h t", h=NH)
        KS1 = KSB[0:ROWS, :].rearrange("p (b h t) -> p b h t", b=B, h=NH)
        HID = KSB[:, 0:NH * TK].bitcast(F32).rearrange("p (a t) -> p a t", a=2)
        PR = sb("PR", [P, NSLOT, CH])
        V1 = sb("V1", [P, NT, NH, 2 * DH])
        V0 = V1[:, 0:TK // P]

        def values_of(n):
            return V1[:, n].rearrange("p h (d w) -> p h d w", w=2)[:, :, :, 0]

        KF = PR[:, 0, :]
        VF = PR[:, 2, :]
        OG = sb("OG", [P, 2, CH])
        MX = sb("MX", [P, 2, 2, 4, 4])
        MR = sb("MR", [P, 4, 4])
        MP = sb("MP", [P, 2, 4, 12], BF16)
        MT = KSB[96:108, 0:2 * CH].rearrange("p (a c) -> p a c", a=2)
        T8 = DEN[0:E, :]
        T8B = PR[0:E, 6:8, :].rearrange("p a c -> p (a c)").bitcast(BF16)

        ident = sb("ident", [P, P])
        identb = sb("identb", [P, P], BF16)
        onesb = sb("onesb", [P, P], BF16)
        trib = sb("trib", [P, P], BF16)
        maskb = sb("maskb", [P, P], BF16)
        expandb = sb("expandb", [E, 2 * P], BF16)
        prio = sb("prio", [P, E])

        Wg0 = sb("Wg0", [P, E])
        Wg1 = sb("Wg1", [P, E])
        gb0 = sb("gb0", [P, E])
        gb1 = sb("gb1", [P, E])
        W1 = sb("W1", [P, E, SUB])
        b1c = sb("b1c", [P, 2])
        W2 = sb("W2", [P, 2, D])
        b2r = sb("b2r", [E, D])
        We = sb("We", [P, E, D])
        ber = sb("ber", [E, D])
        Wqkv = PR[:, 7, 0:3 * D]
        Wo = sb("Wo", [P, D])
        qsc = sb("qsc", [P, 1])
        ksc = sb("ksc", [P, 1])
        Wraw = XT[:, 0:3 * D].rearrange("p (w d) -> p w d", w=3)
        bvr = OG[:, 0, 3 * D:4 * D]
        PARTS = (DEN[:, 2 * CH:2 * CH + 3 * CH // 2].bitcast(BF16).rearrange("p (q c) -> p q c", q=3),
                 XN[:, :, :].rearrange("p n d -> p (n d)")[:, 2 * CH:2 * CH + 3 * CH // 2].bitcast(BF16)
                 .rearrange("p (q c) -> p q c", q=3))
        QF1 = XN[:, :, :].rearrange("p n d -> p (n d)")[:, 0:2 * CH].rearrange("p (w c) -> p w c", w=2)
        KVraw = XT[:, 2 * CH:4 * CH].rearrange("p (a c) -> p a c", a=2)
        WT = OG[:, 0, 0:3 * D].rearrange("p (w d) -> p w d", w=3)
        bqc = sb("bqc", [P, 1])
        bkc = sb("bkc", [P, 1])
        KVT = DEN[:, 0:2 * TK].rearrange("p (a t) -> p a t", a=2)

        st6 = sb("st6", [P, NT, 6])
        st6b = OG[:, 0, 0:12 * NT].rearrange("p (n w c) -> p n w c", n=NT, w=2)
        mvb = sb("mvb", [P, NT, 2, 2])
        rsb = sb("rsb", [P, NT, 2])
        mv = mvb[:, :, 0, :]
        rstd = rsb[:, :, 0]
        RQ = sb("RQ", [P, 3, NT])
        G, G2, GE, EQ = (OG[:, 1, i * NT * E:(i + 1) * NT * E].rearrange("p (n e) -> p n e", e=E) for i in range(4))
        SEL = sb("SEL", [P, NT, E])
        r16 = sb("r16", [P, NT])
        den8 = PR[:, 0, P:P + J * E].rearrange("p (j e) -> p j e", j=J)
        RT = OG[:, 0, 3 * D:4 * D].rearrange("p (b e j) -> p b e j", b=B, e=E)
        PT = PR[:, 0, 0:NT * E].rearrange("p (b e j) -> p b e j", b=B, e=E)
        CA, CB = (PR[:, 1 + i, 0:NT * E // 2].bitcast(BF16).rearrange("p (b e j) -> p b e j", b=B, e=E) for i in range(2))
        thr, cand, took = (RQ[:, i, :] for i in range(3))
        bit = PR[:, 3, 0:NT].bitcast(U32)
        steps = PR[:, 3, NT:NT + 1].bitcast(I32)
        b2tmp = PR[0:E, 3, P:2 * P]
        b2parts = PR[0:E, 3, 2 * P:2 * P + 3 * P // 2].bitcast(BF16).rearrange("p (q d) -> p q d", q=3)

        scrA = nc.dram_tensor("scr_k0", [P, 3, TK], BF16, kind="Internal").ap()
        scrQ0 = nc.dram_tensor("scr_q0", [P, 3, B * S], BF16, kind="Internal").ap()
        scrQ1 = nc.dram_tensor("scr_q1", [P, 3, B * S], BF16, kind="Internal").ap()
        scrK1 = nc.dram_tensor("scr_k1", [P, 3, B * S], BF16, kind="Internal").ap()

        PS = [ctx.enter_context(nc.psum_tensor(f"PS{i}", [P, 2 * CH], F32)) for i in range(4)]

        def bank(i):
            return PS[i // 2][:, (i % 2) * CH:(i % 2 + 1) * CH]

        def score_bank(n):
            return bank((4, 5, 7)[n % 3])

        def expert_bank(n, a):
            return bank((4, 6, 0)[n % 3] + a)

        sems = {}

        def sm(name):
            if name not in sems:
                sems[name] = sem(name)
            return sems[name]

        block = ctx.enter_context(nc.Block())

        PLAN = [attention_plan(False), attention_plan(True)]
        RING_ITEMS = [{"M": 1, "T": 1}, {"M": 1, "T": 1, "Q": 2}]

        def ring_steps(a):
            return [st for st in PLAN[a] for _ in range(RING_ITEMS[a].get(st[0], 0))]

        def shift_item(a, u):
            return ring_base(a) + ring_steps(a).index(("T", u))

        def ring_base(a):
            return 2 * a

        N_CONST = 4 + 1 + 1 + E + 1

        @block.sync
        def _(sp):
            def load(dst, src, s):
                sp.dma_start(dst, src).then_inc(sm(s), 16)

            for b in range(B):
                load(X[:, b * J:(b + 1) * J, :], A["L0_attn_queries"][b].rearrange("(p j) d -> p j d", j=J), f"x_in{b}")
            load(Wraw[:, 0, :], A["L0_attn_Wq_w"], "kv_in")
            load(Wraw[:, 1, :], A["L0_attn_Wk_w"], "kv_in")
            load(Wraw[:, 2, :], A["L0_attn_Wv_w"], "kv_in")
            load(KVraw[:, 0, :].rearrange("p (t d) -> p t d", d=D), A["L0_attn_keys"][0].rearrange("(t p) d -> p t d", p=P), "kv_in")
            load(KVraw[:, 1, :].rearrange("p (t d) -> p t d", d=D), A["L0_attn_values"][0].rearrange("(t p) d -> p t d", p=P), "kv_in")
            load(bqc[:, :], A["L0_attn_Wq_b"].rearrange("(p o) -> p o", o=1), "kv_in")
            load(bkc[:, :], A["L0_attn_Wk_b"].rearrange("(p o) -> p o", o=1), "kv_in")
            load(bvr[:, :], A["L0_attn_Wv_b"].rearrange("(o d) -> o d", o=1).to_broadcast([P, D]), "kv_in")
            load(Wg0[:, :], A["L0_ffn_w_gate_w"], "f0_in")
            load(gb0[:, :], A["L0_ffn_w_gate_b"].rearrange("(o d) -> o d", o=1).to_broadcast([P, E]), "f0_in")
            load(W1[:, :, :], A["L0_ffn_W1"].rearrange("e d h -> d e h"), "f0_in")
            for a in range(2):
                load(b1c[:, a:a + 1], A["L0_ffn_b1"][4 * a:4 * a + 4].rearrange("e h -> (e h)").rearrange("(p o) -> p o", o=1), "f0_in")
            load(W2[:, :, :], A["L0_ffn_W2"].rearrange("e h d -> (e h) d").rearrange("(a p) d -> p a d", p=P), "f0_in")
            load(b2r[:, :], A["L0_ffn_b2"], "f0_in")
            load(Wg1[:, :], A["L1_ffn_Wg"], "f1_in")
            load(gb1[:, :], A["L1_ffn_bg"].rearrange("(o d) -> o d", o=1).to_broadcast([P, E]), "f1_in")
            load(We[:, :, :], A["L1_ffn_We"].rearrange("e d o -> d e o"), "f1_in")
            load(ber[:, :], A["L1_ffn_be"], "f1_in")
            load(Wo[:, :], A["L1_attn_W_out"], "a1_in")
            load(qsc[:, :], A["L1_attn_q_scale"].rearrange("(p o) -> p o", o=1), "a1_in")
            load(ksc[:, :], A["L1_attn_k_scale"].rearrange("(p o) -> p o", o=1), "a1_in")

            def stack(dst, scr, by_part, s, parts=range(3)):
                for a in parts:
                    for c in range(3):
                        r = DH * (3 * a + c)
                        load(dst[r:r + DH], scr.rearrange("(h d) q s -> d q h s", h=NH)[:, a if by_part else c], s)

            def attention_dma(a):
                units = attention_units()

                def scratch(c):
                    here = slice(c * CH, (c + 1) * CH)
                    if a == 0:
                        sp.wait_ge(sm("parts0"), c + 1)
                        load(scrQ0[:, :, here], PARTS[0], f"scr0_{c}")
                        return
                    sp.wait_ge(sm("parts1"), 2 * c + 1)
                    load(scrQ1[:, :, here], PARTS[0], f"scr1_{2 * c}")
                    sp.wait_ge(sm("parts1"), 2 * c + 2)
                    load(scrK1[:, :, here], PARTS[1], f"scr1_{2 * c + 1}")

                def stack_third(c, third):
                    b, cols = c // 2, slice((c % 2) * CH, (c % 2 + 1) * CH)
                    here = slice(c * CH, (c + 1) * CH)
                    if a == 0:
                        sp.wait_ge(sm(f"scr0_{c}"), 16)
                        stack(QS[:, b, :, cols], scrQ0[:, :, here], True, f"qstack0_{c}", (third,))
                        return
                    sp.wait_ge(sm(f"scr1_{2 * c}"), 16)
                    stack(QS[:, b, :, cols], scrQ1[:, :, here], True, f"qstack1_{c}", (third,))
                    sp.wait_ge(sm(f"scr1_{2 * c + 1}"), 16)
                    sp.wait_ge(sm("ks_ones"), 2)
                    stack(KS1[:, b, :, cols], scrK1[:, :, here], False, f"kstack1_{c}", (third,))

                def shift_rows(u):
                    b, c, g = units[u]
                    sp.wait_ge(sm(f"mxfree{a}"), shift_item(a, u) + 1)
                    load(QS[SHIFT_ROW:SHIFT_ROW + 3, b, 4 * g:4 * g + 4, c * CH:(c + 1) * CH],
                         MT[:, u % 2, :], f"mrow{a}_{u % 2}")

                def heads_out(u):
                    b, c, g = units[u]
                    sp.wait_ge(sm(f"og{a}"), u + 1)
                    cols = slice(b * S + c * CH, b * S + (c + 1) * CH)
                    for i in range(4):
                        h = 4 * g + i
                        load(XD[DH * h:DH * h + DH, :, cols], OG[32 * i:32 * i + 2 * DH, u % 2, :], f"ogout{a}_{u % 2}")

                scratch(0)
                for third in range(3):
                    stack_third(0, third)
                for step in PLAN[a]:
                    if step[0] == "Q" and a == 0 or step[0] == "R" and step[2] == 7:
                        scratch(step[1])
                    elif step[0] == "T":
                        u = step[1]
                        shift_rows(u)
                        for c, third in STACK_BEHIND[a].get(u, ()):
                            stack_third(c, third)
                    elif step[0] == "O":
                        heads_out(step[1])

            sp.wait_ge(sm("k0_parts"), 1)
            load(scrA, PARTS[0], "k0_scr")
            sp.wait_ge(sm("k0_scr"), 16)
            sp.wait_ge(sm("ks_ones"), 1)
            stack(KS0, scrA, False, "k0_stack")
            attention_dma(0)
            sp.wait_ge(sm("xadd2"), NCH)
            load(Wqkv, A["L1_attn_W_qkv"], "wqkv_in")
            attention_dma(1)
            for b in range(B):
                sp.wait_ge(sm("xadd5"), NCH // B * (b + 1))
                load(out[b].rearrange("(p j) d -> p j d", j=J), X[:, b * J:(b + 1) * J, :], "stored")
            sp.wait_ge(sm("stored"), 16 * B)

        @block.gpsimd
        def _(pool):
            pool.memset(ident[:, :], 0.0).then_inc(sm("c_set"), 1)
            pool.memset(identb[:, :], 0.0).then_inc(sm("c_set"), 1)
            pool.memset(trib[:, :], 1.0).then_inc(sm("c_set"), 1)
            pool.memset(maskb[:, :], MASKED).then_inc(sm("c_set"), 1)
            pool.memset(expandb[:, :], 1.0).then_inc(sm("c_set"), 1)
            pool.wait_ge(sm("c_set"), 5)
            for m in (ident, identb):
                pool.affine_select(out=m[:, :], in_=m[:, :], compare_op=ALU.not_equal, fill=1.0, base=0,
                                   pattern=[[-1, P]], channel_multiplier=1).then_inc(sm("consts"), 1)
            pool.affine_select(out=trib[:, :], in_=trib[:, :], compare_op=ALU.is_gt, fill=0.0, base=0,
                               pattern=[[1, P]], channel_multiplier=-1).then_inc(sm("consts"), 1)
            pool.affine_select(out=maskb[:, :], in_=maskb[:, :], compare_op=ALU.is_gt, fill=0.0, base=0,
                               pattern=[[1, P]], channel_multiplier=-1).then_inc(sm("consts"), 1)
            pool.affine_select(out=expandb[:, :], in_=expandb[:, :], compare_op=ALU.is_ge, fill=0.0, base=0,
                               pattern=[[1, 2 * P]], channel_multiplier=-SUB).then_inc(sm("c_set"), 1)
            pool.wait_ge(sm("c_set"), 6)
            pool.affine_select(out=expandb[:, :], in_=expandb[:, :], compare_op=ALU.is_ge, fill=0.0, base=SUB - 1,
                               pattern=[[-1, 2 * P]], channel_multiplier=SUB).then_inc(sm("consts"), 1)
            pool.memset(onesb[:, :], 1.0).then_inc(sm("consts"), 1)
            for e in range(E):
                pool.memset(prio[:, e:e + 1], float(E - e)).then_inc(sm("consts"), 1)
            pool.wait_ge(sm("consts"), 4 + 1 + 1 + E)
            pool.memset(KSB[64:96, NH * TK:2 * NH * TK], 1.0).then_inc(sm("ks_ones"), 1)
            pool.wait_ge(sm("ks_ones"), 1)
            pool.memset(V1[:, :, :, :], 1.0).then_inc(sm("consts"), 1)

            XNf = XN[:, :, :].rearrange("p n d -> p (n d)")
            Xf = X[:, :, :].rearrange("p n d -> p (n d)")

            pool_chain = [0]

            def link(ins):
                pool_chain[0] += 1
                ins.then_inc(sm("pool_chain"), 1)
                pool.wait_ge(sm("pool_chain"), pool_chain[0])

            pool.wait_ge(sm("xn1"), NT)
            for c in range(NCH):
                cols = slice(c * CH, (c + 1) * CH)
                link(pool.tensor_tensor(Xf[:, cols], Xf[:, cols], XNf[:, cols], ALU.add))
            for step in PLAN[0]:
                if step[0] == "Q":
                    c = step[1]
                    pool.wait_ge(sm("qf0"), c + 1)
                    pool.wait_ge(sm(f"scr0_{c - 1}"), 16)
                    src, dst = XT[:, c * CH:(c + 1) * CH], PARTS[0]
                    link(pool.tensor_copy(dst[:, 0, :], src))
                    link(pool.tensor_tensor(src, src, dst[:, 0, :], ALU.subtract))
                    link(pool.tensor_copy(dst[:, 1, :], src))
                    pool.tensor_tensor(dst[:, 2, :], src, dst[:, 1, :], ALU.subtract).then_inc(sm("parts0"), 1)
                elif step[0] == "F" and step[1:3] != (B - 1, S // CH - 1) and step[3] == FP - 1:
                    c = step[1] * (S // CH) + step[2]
                    cols = slice(c * CH, (c + 1) * CH)
                    pool.wait_ge(sm("rden0"), FP * (c + 1))
                    link(pool.tensor_tensor(NUM[:, cols], NUM[:, cols], DEN[:, cols], ALU.mult))
                    pool.tensor_tensor(Xf[:, cols], Xf[:, cols], NUM[:, cols], ALU.add).then_inc(sm("x_attn0"), 1)

            pool.wait_ge(sm("consts"), N_CONST)
            pool.wait_ge(sm("xadd2"), NCH)
            pool.memset(KSB[64:96, :], 1.0).then_inc(sm("ks_ones"), 1)
            pool.wait_ge(sm("ks_ones"), 2)
            n = 0
            for step in PLAN[1]:
                if step[0] != "E":
                    continue
                tt, off, diag = exp_groups(attention_units()[step[1]], True)[step[2]]
                if diag:
                    pool.wait_ge(sm("p1"), n + 1)
                    blk = PR[:, n % NSLOT, off:off + P]
                    pool.affine_select(out=blk, in_=blk, compare_op=ALU.is_ge, fill=0.0, base=0,
                                       pattern=[[1, P]], channel_multiplier=-1).then_inc(sm("pmask"), 1)
                n += 1

        @block.tensor
        def _(pe):
            def transpose_x(k):
                if k == 0:
                    pe.wait_ge(sm("wt"), 3)
                    pe.wait_ge(sm("kf"), 1)
                for n in range(NT):
                    q = n // 4
                    pe.wait_ge(sm(f"xn{k}"), n + 1)
                    if q >= 2 and n % 4 == 0:
                        pe.wait_ge(sm(f"xt{k}"), q - 1)
                    pe.transpose(bank(q % 2)[:, (n % 4) * P:(n % 4 + 1) * P], XN[:, n, :], ident[:, :])\
                        .then_inc(sm(f"xtp{k}"), 1)

            def gates(k, Wg):
                for n in range(NT):
                    pe.wait_ge(sm(f"xt{k}"), n // 4 + 1)
                    mm = pe.matmul(bank(2)[:, n * E:(n + 1) * E], XT[:, n * P:(n + 1) * P], Wg[:, :], start=True, stop=True)
                mm.then_inc(sm(f"lg{k}"), 1)

            def transpose_sel(k):
                pe.wait_ge(sm(f"sel{k}"), 2 if k in (0, 2) else 1)
                for n in range(NT):
                    q = n // 4
                    if q >= 2 and n % 4 == 0:
                        pe.wait_ge(sm(f"t8{k}"), q - 1)
                    mm = pe.transpose(bank(2 + q % 2)[0:E, (n % 4) * P:(n % 4 + 1) * P], SEL[:, n, :], ident[:, :])
                    if n % 4 == 3:
                        mm.then_inc(sm(f"t8p{k}"), 1)

            def ffn0(k):
                transpose_x(k)
                pe.wait_ge(sm("f0_in"), 16 * 7)
                gates(k, Wg0)
                if k == 0:
                    pe.wait_ge(sm("vf"), 1)
                n = 0
                for q in range(NCH):
                    for a in range(2):
                        if n >= 4:
                            pe.wait_ge(sm(f"hid{k}"), n - 3)
                        pe.matmul(bank(4 + n % 4), W1[:, 4 * a:4 * a + 4, :].rearrange("p e h -> p (e h)"),
                                  XT[:, q * CH:(q + 1) * CH], start=True, stop=True).then_inc(sm(f"hidp{k}"), 1)
                        n += 1
                def count_tokens():
                    for j in range(J):
                        mm = pe.matmul(bank(3)[:, 0:NT], onesb[:, :], CA[:, :, :, j].rearrange("p b e -> p (b e)"),
                                       start=(j == 0), stop=(j == J - 1))
                    mm.then_inc(sm(f"cnt{k}"), 1)

                pe.wait_ge(sm(f"cmp{k}"), 1)
                count_tokens()
                pe.wait_ge(sm(f"steps{k}"), 1)
                with pe.Fori(0, pe.value_load(steps[0:1, 0:1], min_val=0, max_val=RB)) as r:
                    pe.wait_ge(sm(f"cmp{k}"), r + 2)
                    count_tokens()
                pe.wait_ge(sm(f"gteq{k}"), 2)
                rank = bank(3)[:, 0:NT * J].rearrange("p (n j) -> p n j", j=J)
                for j in range(J):
                    gt = CA[:, :, :, j].rearrange("p b e -> p (b e)").unsqueeze(2).to_broadcast([P, NT, J])
                    eq = CB[:, :, :, j].rearrange("p b e -> p (b e)").unsqueeze(2)
                    pe.matmul(rank, onesb[:, :], gt, start=(j == 0), stop=False)
                    mm = pe.matmul(rank, trib[:, :], eq.to_broadcast([P, NT, J]), start=False, stop=(j == J - 1))
                    if j < J - 1:
                        pe.matmul(rank[:, :, j + 1:J], identb[:, :], eq.to_broadcast([P, NT, J - 1 - j]),
                                  start=False, stop=False)
                mm.then_inc(sm(f"rank{k}"), 1)
                transpose_sel(k)
                n = 0
                for q in range(NCH):
                    pe.wait_ge(sm(f"t8{k}"), q + 1)
                    for a in range(2):
                        if n >= 4:
                            pe.wait_ge(sm(f"hm{k}"), n - 3)
                        pe.matmul(bank(4 + n % 4), expandb[:, a * P:(a + 1) * P], T8B[:, q * CH:(q + 1) * CH],
                                  start=True, stop=True).then_inc(sm(f"spread{k}"), 1)
                        n += 1
                for n in range(NT):
                    q = n // 4
                    if n % 4 == 0:
                        pe.wait_ge(sm(f"hm{k}"), 2 * q + 2)
                        pe.wait_ge(sm(f"t8{k}"), NCH)
                        if q == 0:
                            pe.wait_ge(sm(f"b2p{k}"), 1)
                        if q >= 2:
                            pe.wait_ge(sm(f"xadd{k}"), q - 1)
                    dst = bank(2 + q % 2)[:, (n % 4) * P:(n % 4 + 1) * P]
                    cols = slice(n * P, (n + 1) * P)
                    pe.matmul(dst, HID[:, 0, cols], W2[:, 0, :], start=True, stop=False)
                    pe.matmul(dst, HID[:, 1, cols], W2[:, 1, :], start=False, stop=False)
                    for part in range(3):
                        mm = pe.matmul(dst, T8B[:, cols], b2parts[:, part, :], start=False, stop=part == 2)
                    mm.then_inc(sm(f"y{k}"), 1)

            def ffn1(k):
                transpose_x(k)
                if k == 3:
                    pe.wait_ge(sm("f1_in"), 16 * 4)
                gates(k, Wg1)
                for n in range(NT):
                    if n >= 3:
                        pe.wait_ge(sm(f"comb{k}"), n - 2)
                    for a in range(2):
                        mm = pe.matmul(expert_bank(n, a), XT[:, n * P:(n + 1) * P],
                                       We[:, 4 * a:4 * a + 4, :].rearrange("p e o -> p (e o)"), start=True, stop=True)
                    mm.then_inc(sm(f"ye{k}"), 1)
                    if n == 2:
                        transpose_sel(k)
                    if n in (4, 5, 8, 12):
                        q = (4, 5, 8, 12).index(n)
                        pe.wait_ge(sm(f"t8{k}"), NCH)
                        if q >= 2:
                            pe.wait_ge(sm(f"xadd{k}"), q - 1)
                        for m in range(4 * q, 4 * q + 4):
                            pe.matmul(bank(2 + q % 2)[:, (m % 4) * P:(m % 4 + 1) * P], T8[:, m * P:(m + 1) * P], ber[:, :],
                                      start=True, stop=True).then_inc(sm(f"y{k}"), 1)

            def keys_values():
                pe.wait_ge(sm("consts"), N_CONST)
                pe.wait_ge(sm("kv_in"), 16 * 8)
                for w in range(3):
                    mm = pe.transpose(bank(0)[:, w * P:(w + 1) * P], Wraw[:, w, :], ident[:, :])
                mm.then_inc(sm("wtp"), 1)
                for a in range(2):
                    for t in range(4):
                        mm = pe.transpose(bank(1 + a)[:, t * P:(t + 1) * P], KVraw[:, a, t * P:(t + 1) * P], ident[:, :])
                    mm.then_inc(sm("wtp"), 1)
                pe.wait_ge(sm("wt"), 2)
                pe.matmul(bank(3), WT[:, 1, :], KVT[:, 0, :], start=True, stop=True).then_inc(sm("kp"), 1)
                pe.wait_ge(sm("wt"), 3)
                for t in range(4):
                    mm = pe.matmul(bank(4)[:, t * P:(t + 1) * P], KVT[:, 1, t * P:(t + 1) * P], WT[:, 2, :],
                                   start=True, stop=True)
                mm.then_inc(sm("vp"), 1)

            def attention(a, k):
                units = attention_units()
                transpose_x(k)
                pe.wait_ge(sm(f"xt{k}"), NCH)
                if a == 0:
                    for c in range(NCH):
                        if c >= 2:
                            pe.wait_ge(sm("qf0"), c - 1)
                        pe.matmul(bank(4 + c % 2), WT[:, 0, :], XT[:, c * CH:(c + 1) * CH], start=True, stop=True)\
                            .then_inc(sm("qp0"), 1)
                    pe.wait_ge(sm("k0_stack"), 16 * 9)
                else:
                    pe.wait_ge(sm("a1_in"), 16 * 3)
                    pe.wait_ge(sm("wqkv_in"), 16)
                    for n in range(NT):
                        if n >= 4:
                            pe.wait_ge(sm("v1"), 2 * (n - 3))
                        pe.matmul(bank(4 + n % 4)[:, 0:3 * D], XT[:, n * P:(n + 1) * P], Wqkv,
                                  start=True, stop=True).then_inc(sm("qkvp"), 1)

                KSof = (lambda b: KS0) if a == 0 else (lambda b: KS1[:, b])
                Vof = (lambda b, tt: V0[:, tt]) if a == 0 else (lambda b, tt: V1[:, b * J + tt])
                m = 0
                n = 0
                pv = 0
                diags = 0

                def ring_bank():
                    if m >= 4:
                        pe.wait_ge(sm(f"mxfree{a}"), m - 3)
                    return bank(m % 4)

                def transpose_qk(c):
                    nonlocal m
                    pe.wait_ge(sm("qkn"), 8 * (c + 1))
                    for w in range(2):
                        dst = ring_bank()
                        for t in range(4):
                            mm = pe.transpose(dst[:, t * P:(t + 1) * P], RAW[:, 4 * c + t, w, :], ident[:, :])
                        mm.then_inc(sm(f"mxp{a}"), 1)
                        m += 1

                if a == 1:
                    transpose_qk(0)

                def project(b):
                    for n in range(b * J, (b + 1) * J):
                        q, j = n // 4, n % J
                        if n % 4 == 0:
                            pe.wait_ge(sm("ctx"), FP * (2 * b + 2))
                            if q >= 2:
                                pe.wait_ge(sm(f"xadd{k}"), q - 1)
                            else:
                                pe.wait_ge(sm(f"mxfree{a}"), m)
                        pe.matmul(bank(2 + q % 2)[:, (n % 4) * P:(n % 4 + 1) * P],
                                  NUM[:, b * S:(b + 1) * S].rearrange("p (s j) -> p j s", j=J)[:, j, :], Wo[:, :],
                                  start=True, stop=True).then_inc(sm(f"y{k}"), 1)

                stacked = -1
                for step in PLAN[a]:
                    if step[0] == "M":
                        (b, c, g), (st, t0, w, i0, nh) = units[step[1]], step[2]
                        while stacked < 2 * b + c:
                            stacked += 1
                            pe.wait_ge(sm(f"qstack{a}_{stacked}"), 16 * 9)
                            if a == 1:
                                pe.wait_ge(sm(f"kstack1_{stacked}"), 16 * 9)
                        dst = ring_bank()
                        s0 = c * CH + st * P
                        diag = a == 1 and t0 == c * CH
                        for i in range(i0, i0 + nh):
                            o = (i - i0) * w
                            mm = pe.matmul(dst[:, o:o + w], QS[0:SHIFT_ROW, b, 4 * g + i, s0:s0 + P],
                                           KSof(b)[0:SHIFT_ROW, 4 * g + i, t0:t0 + w], start=True, stop=not diag)
                            if diag:
                                mm = pe.matmul(dst[:, o + w - P:o + w], identb[:, :], maskb[:, :], start=False, stop=True)
                        mm.then_inc(sm(f"mxp{a}"), 1)
                        m += 1
                    elif step[0] == "T":
                        u = step[1]
                        pe.wait_ge(sm(f"mp{a}"), u + 1)
                        dst = ring_bank()[0:12, 0:CH // 2].bitcast(BF16)
                        for st in range(4):
                            mm = pe.transpose(dst[:, st * P:(st + 1) * P], MP[:, u % 2, st, :], identb[:, :])
                        mm.then_inc(sm(f"mxp{a}"), 1)
                        m += 1
                    elif step[0] == "Q" and a == 1:
                        transpose_qk(step[1])
                    elif step[0] == "E":
                        _, u, k2, i = step
                        (b, c, g), (tt, off, diag) = units[u], exp_groups(units[u], a)[k2]
                        if k2 == 0 and i == 0:
                            pe.wait_ge(sm(f"mrow{a}_{u % 2}"), 16 * (u // 2 + 1))
                        if n >= 3:
                            pe.wait_ge(sm(f"p{a}"), n - 2)
                        elif a == 0:
                            pe.wait_ge(sm("qf0"), NCH)
                        else:
                            pe.wait_ge(sm("v1"), 2 * NT)
                        pe.matmul(score_bank(n)[:, 0:CH - off], KSof(b)[0:ROWS, 4 * g + i, tt * P:(tt + 1) * P],
                                  QS[0:ROWS, b, 4 * g + i, c * CH + off:(c + 1) * CH], start=True, stop=True)\
                            .then_inc(sm(f"sc{a}"), 1)
                        n += 1
                    elif step[0] == "Y":
                        project(0)
                    elif step[0] == "V":
                        _, u, k2 = step
                        groups = exp_groups(units[u], a)
                        (b, c, g), (tt, off, diag) = units[u], groups[k2]
                        if k2 == 0 and u >= 1:
                            pe.wait_ge(sm(f"og{a}"), u)
                        if a == 1 and diag:
                            diags += 4
                            pe.wait_ge(sm("pmask"), diags)
                        pe.wait_ge(sm(f"p{a}"), pv + 4)
                        for i in range(4):
                            pe.matmul(bank(6)[32 * i:32 * i + 2 * DH, off:CH], Vof(b, tt)[:, 4 * g + i, :],
                                      PR[:, pv % NSLOT, off:CH], start=k2 == 0, stop=k2 == len(groups) - 1)\
                                .then_inc(sm(f"pv{a}"), 1)
                            pv += 1
                if a == 1:
                    project(B - 1)

            keys_values()
            ffn0(0)
            attention(0, 1)
            ffn0(2)
            ffn1(3)
            attention(1, 4)
            ffn1(5)

        @block.scalar
        def _(act):
            def copy_xt(k, natural):
                for q in range(NCH):
                    act.wait_ge(sm(f"xtp{k}"), 4 * q + 4)
                    if natural:
                        b, j0 = q // 2, 4 * (q % 2)
                        dst = XT[:, b * S:(b + 1) * S].rearrange("d (p j) -> d j p", j=J)[:, j0:j0 + 4, :]
                        src = bank(q % 2).rearrange("d (j p) -> d j p", p=P)
                    else:
                        dst, src = XT[:, q * CH:(q + 1) * CH], bank(q % 2)
                    act.activation(dst, src, ACT.Copy).then_inc(sm(f"xt{k}"), 1)

            def gate_exp(k):
                act.wait_ge(sm(f"gsub{k}"), 1)
                act.activation(GE, G, ACT.Exp).then_inc(sm(f"gexp{k}"), 1)

            def copy_t8(k):
                for q in range(NCH):
                    act.wait_ge(sm(f"t8p{k}"), q + 1)
                    dst = (T8B if k in (0, 2) else T8)[:, q * CH:(q + 1) * CH]
                    act.activation(dst, bank(2 + q % 2)[0:E, :], ACT.Copy).then_inc(sm(f"t8{k}"), 1)

            def ffn0(k):
                copy_xt(k, False)
                gate_exp(k)
                n = 0
                for q in range(NCH):
                    for a in range(2):
                        act.wait_ge(sm(f"hidp{k}"), n + 1)
                        act.activation(HID[:, a, q * CH:(q + 1) * CH], bank(4 + n % 4), ACT.Gelu, bias=b1c[:, a:a + 1])\
                            .then_inc(sm(f"hid{k}"), 1)
                        n += 1
                copy_t8(k)

            def ffn1(k):
                copy_xt(k, False)
                gate_exp(k)
                copy_t8(k)

            def attention(a, k):
                units = attention_units()
                copy_xt(k, True)
                if a == 0:
                    for c in range(NCH):
                        act.wait_ge(sm("qp0"), c + 1)
                        act.activation(XT[:, c * CH:(c + 1) * CH], bank(4 + c % 2), ACT.Relu, bias=bqc[:, 0:1]).then_inc(sm("qf0"), 1)
                else:
                    for n in range(NT):
                        act.wait_ge(sm("qkvp"), n + 1)
                        act.activation(RAW[:, n], bank(4 + n % 4)[:, 0:2 * D].rearrange("p (w d) -> p w d", w=2), ACT.Copy)\
                            .then_inc(sm("v1"), 1)
                        act.activation(values_of(n), bank(4 + n % 4)[:, 2 * D:3 * D].rearrange("p (h d) -> p h d", h=NH),
                                       ACT.Copy).then_inc(sm("v1"), 1)
                n = 0
                sums = 0
                for step in PLAN[a]:
                    if step[0] == "E":
                        off = exp_groups(units[step[1]], a)[step[2]][1]
                        act.wait_ge(sm(f"sc{a}"), n + 1)
                        if n >= NSLOT:
                            act.wait_ge(sm(f"pv{a}"), n - NSLOT + 1)
                        act.activation(PR[:, n % NSLOT, off:CH], score_bank(n)[:, 0:CH - off], ACT.Exp)\
                            .then_inc(sm(f"p{a}"), 1)
                        n += 1
                    elif step[0] == "O":
                        u = step[1]
                        sums += 4 * len(exp_groups(units[u], a))
                        act.wait_ge(sm(f"pv{a}"), sums)
                        if u >= 2:
                            act.wait_ge(sm(f"ogout{a}_{u % 2}"), 64 * (u // 2))
                        act.activation(OG[:, u % 2, :], bank(6), ACT.Copy).then_inc(sm(f"og{a}"), 1)

            act.wait_ge(sm("wtp"), 1)
            act.activation(WT[:, :, :].rearrange("p w d -> p (w d)"), bank(0)[:, 0:3 * P], ACT.Copy).then_inc(sm("wt"), 1)
            for a in range(2):
                act.wait_ge(sm("wtp"), 2 + a)
                act.activation(KVT[:, a, :], bank(1 + a), ACT.Copy).then_inc(sm("wt"), 1)
            act.wait_ge(sm("kp"), 1)
            act.activation(KF, bank(3), ACT.Relu, bias=bkc[:, 0:1]).then_inc(sm("kf"), 1)
            ffn0(0)
            attention(0, 1)
            ffn0(2)
            ffn1(3)
            attention(1, 4)
            ffn1(5)

        @block.vector
        def _(dve):
            chain = [0]

            def link(ins):
                chain[0] += 1
                ins.then_inc(sm("dve_chain"), 1)
                dve.wait_ge(sm("dve_chain"), chain[0])

            def mark(ins):
                chain[0] += 1
                ins.then_inc(sm("dve_chain"), 1)

            def settle():
                dve.wait_ge(sm("dve_chain"), chain[0])

            def rsqrt(dst, src, eps):
                a, y, t = (RQ[:, i, 0:src.shape[-1]] for i in range(3))
                link(dve.tensor_scalar(a, src, eps, None, ALU.add))
                link(dve.tensor_scalar(t.bitcast(I32), a.bitcast(I32), 1, None, ALU.logical_shift_right))
                link(dve.tensor_scalar(y.bitcast(I32), t.bitcast(I32), -1.0, float(0x5f3759df), ALU.mult, ALU.add))
                for step in range(3):
                    link(dve.scalar_tensor_tensor(out=t, in0=y, scalar=-0.5, in1=y, op0=ALU.mult, op1=ALU.mult))
                    link(dve.tensor_tensor(t, t, a, ALU.mult))
                    link(dve.scalar_tensor_tensor(out=(dst if step == 2 else y), in0=t, scalar=1.5, in1=y,
                                                  op0=ALU.add, op1=ALU.mult))

            def moments(q):
                for n in range(4 * q, 4 * q + 4):
                    mark(dve.bn_stats(st6[:, n, :], X[:, n, :]))

            def normalise_tiles(k, first, last):
                settle()
                for n in range(first, last):
                    mark(dve.bn_aggr(mv[:, n, :], st6[:, n, :]))
                settle()
                rsqrt(rstd[:, first:last], mv[:, first:last, 1], 1e-5)
                for n in range(first, last):
                    dve.tensor_scalar(XN[:, n, :], X[:, n, :], mv[:, n, 0:1], rstd[:, n:n + 1], ALU.subtract, ALU.mult)\
                        .then_inc(sm(f"xn{k}"), 1)
                dve.wait_ge(sm(f"xn{k}"), last)

            def layernorm(k):
                settle()
                if k == 0:
                    for b in range(B):
                        dve.wait_ge(sm(f"x_in{b}"), 16)
                        moments(2 * b)
                        moments(2 * b + 1)
                        normalise_tiles(k, b * J, (b + 1) * J)
                    return
                for q in range(NCH):
                    moments(q)
                normalise_tiles(k, 0, NT)

            def wide(t):
                return t[:, :].unsqueeze(2).to_broadcast([P, NT, E])

            def gate_top2(k, gb):
                pri = prio[:, :].unsqueeze(1).to_broadcast([P, NT, E])
                logits = bank(2)[:, 0:NT * E].rearrange("p (n e) -> p n e", e=E)
                dve.wait_ge(sm(f"lg{k}"), 1)
                link(dve.tensor_tensor(G, logits, gb[:, :].unsqueeze(1).to_broadcast([P, NT, E]), ALU.add))
                link(dve.tensor_reduce(r16[:, :], G, AX, ALU.max))
                dve.tensor_tensor(G, G, wide(r16), ALU.subtract).then_inc(sm(f"gsub{k}"), 1)
                dve.wait_ge(sm(f"gexp{k}"), 1)
                link(dve.tensor_reduce(r16[:, :], GE, AX, ALU.add))
                link(dve.reciprocal(r16[:, :], r16[:, :]))
                link(dve.tensor_tensor(G, GE, wide(r16), ALU.mult))
                src = G
                for turn in range(2):
                    link(dve.tensor_reduce(r16[:, :], src[:, :, :], AX, ALU.max))
                    link(dve.tensor_tensor(EQ, src[:, :, :], wide(r16), ALU.is_equal))
                    link(dve.tensor_tensor(EQ, EQ, pri, ALU.mult))
                    link(dve.tensor_reduce(r16[:, :], EQ, AX, ALU.max))
                    if turn == 0:
                        link(dve.tensor_tensor(SEL[:, :, :], EQ, wide(r16), ALU.is_equal))
                        link(dve.scalar_tensor_tensor(out=G2, in0=SEL[:, :, :], scalar=-2.0, in1=G,
                                                      op0=ALU.mult, op1=ALU.add))
                        src = G2
                    else:
                        link(dve.tensor_tensor(EQ, EQ, wide(r16), ALU.is_equal))
                link(dve.tensor_tensor(SEL[:, :, :], SEL[:, :, :], EQ, ALU.add))
                link(dve.tensor_tensor(G2, G, SEL[:, :, :], ALU.mult))

            def ffn0(k):
                if k == 0:
                    layernorm(k)
                    keys_values()
                    dve.wait_ge(sm("f0_in"), 16 * 7)
                link(dve.tensor_copy(b2tmp, b2r[:, :]))
                split(b2tmp, b2parts, f"b2p{k}")
                gate_top2(k, gb0)
                per_b = G2.rearrange("p (b j) e -> p b j e", b=B)
                link(dve.tensor_tensor(den8, per_b[:, 0], per_b[:, 1], ALU.add))
                link(dve.tensor_scalar(den8, den8, 1e-6, None, ALU.add))
                link(dve.reciprocal(den8, den8))
                for b in range(B):
                    mark(dve.tensor_tensor(RT[:, b].rearrange("p e j -> p j e"), per_b[:, b], den8, ALU.mult))
                settle()
                link(dve.tensor_scalar(RT[:, :, :, :], RT[:, :, :, :], float(B), None, ALU.mult))
                route = RT[:, :, :, :].rearrange("p b e j -> p (b e) j")
                CAv = CA[:, :, :, :].rearrange("p b e j -> p (b e) j")
                CBv = CB[:, :, :, :].rearrange("p b e j -> p (b e) j")
                PTv = PT[:, :, :, :].rearrange("p b e j -> p (b e) j")

                def by_row(t):
                    return t[:, :].unsqueeze(2).to_broadcast([P, NT, J])

                dve.tensor_scalar(CAv, route, 0.0, None, ALU.is_gt).then_inc(sm(f"cmp{k}"), 1)
                mark(dve.memset(thr[:, :], 0.0))
                link(dve.memset(bit[:, :], 1 << (RB - 1)))
                dve.wait_ge(sm(f"cnt{k}"), 1)
                link(dve.tensor_reduce(took[:, 0:1], bank(3)[:, 0:NT], AX, ALU.max))
                dve.tensor_scalar(steps[:, :], took[:, 0:1], KTOP + 0.5, float(RB), ALU.is_ge, ALU.mult).then_inc(sm(f"steps{k}"), 1)
                dve.wait_ge(sm(f"steps{k}"), 1)
                with dve.Fori(0, dve.value_load(steps[0:1, 0:1], min_val=0, max_val=RB)) as r:
                    dve.tensor_tensor(cand[:, :].bitcast(U32), thr[:, :].bitcast(U32), bit[:, :], ALU.bitwise_or)\
                        .then_inc(sm(f"search{k}"), 1)
                    dve.wait_ge(sm(f"search{k}"), r * 4 + 1)
                    dve.tensor_tensor(CAv, route, by_row(cand), ALU.is_ge).then_inc(sm(f"cmp{k}"), 1)
                    dve.wait_ge(sm(f"cnt{k}"), r + 2)
                    dve.scalar_tensor_tensor(out=took[:, :], in0=bank(3)[:, 0:NT], scalar=KTOP - 0.5, in1=cand[:, :],
                                             op0=ALU.is_ge, op1=ALU.mult).then_inc(sm(f"search{k}"), 1)
                    dve.wait_ge(sm(f"search{k}"), r * 4 + 2)
                    dve.tensor_scalar(bit[:, :], bit[:, :], 1, None, ALU.logical_shift_right).then_inc(sm(f"search{k}"), 1)
                    dve.tensor_tensor(thr[:, :], thr[:, :], took[:, :], ALU.max).then_inc(sm(f"search{k}"), 1)
                    dve.wait_ge(sm(f"search{k}"), r * 4 + 4)
                link(dve.scalar_tensor_tensor(out=thr[:, :], in0=thr[:, :], scalar=1.2e-38, in1=thr[:, :],
                                              op0=ALU.is_ge, op1=ALU.mult))
                dve.tensor_tensor(CAv, route, by_row(thr), ALU.is_gt).then_inc(sm(f"gteq{k}"), 1)
                dve.tensor_tensor(CBv, route, by_row(thr), ALU.is_equal).then_inc(sm(f"gteq{k}"), 1)
                dve.wait_ge(sm(f"rank{k}"), 1)
                link(dve.scalar_tensor_tensor(out=PTv, in0=bank(3)[:, 0:NT * J].rearrange("p (n j) -> p n j", j=J),
                                              scalar=KTOP - 0.5, in1=CBv, op0=ALU.is_lt, op1=ALU.mult))
                selv = SEL[:, :, :].rearrange("p (b j) e -> p b e j", b=B)
                for b in range(B):
                    dve.tensor_tensor(selv[:, b], PT[:, b], CA[:, b], ALU.add).then_inc(sm(f"sel{k}"), 1)
                n = 0
                for q in range(NCH):
                    for a in range(2):
                        dve.wait_ge(sm(f"spread{k}"), n + 1)
                        dve.wait_ge(sm(f"hid{k}"), n + 1)
                        h = HID[:, a, q * CH:(q + 1) * CH]
                        dve.tensor_tensor(h, h, bank(4 + n % 4), ALU.mult).then_inc(sm(f"hm{k}"), 1)
                        n += 1
                add_back(k, 0.5)

            def add_chunk(k, scale, q):
                dve.wait_ge(sm(f"y{k}"), 4 * q + 4)
                if k in (3, 5):
                    dve.wait_ge(sm(f"comb{k}"), 4 * q + 4)
                x4 = X[:, 4 * q:4 * q + 4, :].rearrange("p n d -> p (n d)")
                src = bank(2 + q % 2)
                dve.scalar_tensor_tensor(out=x4, in0=src, scalar=scale, in1=x4, op0=ALU.mult, op1=ALU.add)\
                    .then_inc(sm(f"xadd{k}"), 1)

            def add_back(k, scale, first=0, last=NCH):
                for q in range(first, last):
                    add_chunk(k, scale, q)
                    dve.wait_ge(sm(f"xadd{k}"), q + 1)
                    moments(q)
                    if q % 2 == 1:
                        normalise_tiles(k + 1, 4 * (q - 1), 4 * (q + 1))

            def ffn1(k):
                gate_top2(k, gb1)
                link(dve.tensor_reduce(r16[:, :], G2, AX, ALU.add))
                link(dve.reciprocal(r16[:, :], r16[:, :]))
                link(dve.tensor_tensor(G2, G2, wide(r16), ALU.mult))
                dve.tensor_scalar(SEL[:, :, :], G2, 0.5, None, ALU.mult).then_inc(sm(f"sel{k}"), 1)
                dve.wait_ge(sm(f"sel{k}"), 1)
                ops = sorted((4 * n + e, n, e) for n in range(NT) for e in range(E))
                added = {}
                for _, n, e in ops:
                    if e == 0:
                        dve.wait_ge(sm(f"ye{k}"), n + 1)
                    else:
                        dve.wait_ge(sm("dve_chain"), added[n])
                    ins = dve.scalar_tensor_tensor(out=X[:, n, :], in0=expert_bank(n, e // 4)[:, (e % 4) * D:(e % 4 + 1) * D],
                                                   scalar=SEL[:, n, e:e + 1], in1=X[:, n, :], op0=ALU.mult, op1=ALU.add)
                    if e < E - 1:
                        mark(ins)
                        added[n] = chain[0]
                    else:
                        ins.then_inc(sm(f"comb{k}"), 1)
                        if n % 4 == 1 and n > 4:
                            add_chunk(k, 1.0, n // 4 - 1)
                add_chunk(k, 1.0, NCH - 1)
                dve.wait_ge(sm(f"xadd{k}"), NCH)
                if k == 3:
                    layernorm(k + 1)

            def split(src, dst, done):
                link(dve.tensor_copy(dst[:, 0, :], src))
                link(dve.tensor_tensor(src, src, dst[:, 0, :], ALU.subtract))
                link(dve.tensor_copy(dst[:, 1, :], src))
                dve.tensor_tensor(dst[:, 2, :], src, dst[:, 1, :], ALU.subtract).then_inc(sm(done), 1)

            def attention(a, k):
                units = attention_units()
                m = 0

                def scale(c):
                    nonlocal m
                    if c >= 1:
                        dve.wait_ge(sm("parts1"), 2 * c)
                    for w in range(2):
                        dve.wait_ge(sm(f"mxp{a}"), m + 1)
                        dve.tensor_scalar(QF1[:, w, :], bank(m % 4), (qsc, ksc)[w][:, 0:1],
                                          (float(DH) ** -0.5, 1.0)[w], ALU.mult, ALU.mult).then_inc(sm(f"mxfree{a}"), 1)
                        m += 1
                    return m

                def split_piece(c, i, scaled, before):
                    src, dst = QF1[:, i // 4, :], PARTS[i // 4]
                    if i == 0:
                        dve.wait_ge(sm(f"mxfree{a}"), scaled)
                    if i % 4 == 0:
                        dve.wait_ge(sm(f"scr1_{2 * (c - 1) + i // 4}"), 16)
                        mark(dve.tensor_copy(dst[:, 0, :], src))
                        return chain[0]
                    dve.wait_ge(sm("dve_chain"), before)
                    if i % 4 == 1:
                        mark(dve.tensor_tensor(src, src, dst[:, 0, :], ALU.subtract))
                    elif i % 4 == 2:
                        mark(dve.tensor_copy(dst[:, 1, :], src))
                    else:
                        dve.tensor_tensor(dst[:, 2, :], src, dst[:, 1, :], ALU.subtract).then_inc(sm("parts1"), 1)
                    return chain[0]

                def prepare(c):
                    nonlocal m
                    if a == 0:
                        dve.wait_ge(sm("qf0"), c + 1)
                        if c >= 1:
                            dve.wait_ge(sm(f"scr0_{c - 1}"), 16)
                        split(XT[:, c * CH:(c + 1) * CH], PARTS[0], "parts0")
                        dve.wait_ge(sm("parts0"), c + 1)
                        return
                    scale(c)
                    dve.wait_ge(sm(f"mxfree{a}"), m)
                    for w in range(2):
                        if c >= 1:
                            dve.wait_ge(sm(f"scr1_{2 * (c - 1) + w}"), 16)
                        split(QF1[:, w, :], PARTS[w], "parts1")
                    dve.wait_ge(sm("parts1"), 2 * c + 2)

                def normalise(c, pieces=range(8)):
                    for i in pieces:
                        n, w = 4 * c + i // 2, i % 2
                        dve.tensor_scalar(RAW[:, n, w, :], RAW[:, n, w, :], mvb[:, n, w, 0:1], rsb[:, n, w:w + 1],
                                          ALU.subtract, ALU.mult).then_inc(sm("qkn"), 1)

                def statistics(b):
                    for n in range(b * J, (b + 1) * J):
                        dve.wait_ge(sm("v1"), 2 * n + 1)
                        for w in range(2):
                            mark(dve.bn_stats(st6b[:, n, w, :], RAW[:, n, w, :]))
                    settle()
                    for n in range(b * J, (b + 1) * J):
                        for w in range(2):
                            mark(dve.bn_aggr(mvb[:, n, w, :], st6b[:, n, w, :]))
                    settle()
                    rsqrt(rsb[:, b * J:(b + 1) * J, :].rearrange("p n w -> p (n w)"),
                          mvb[:, b * J:(b + 1) * J, :, 1].rearrange("p n w -> p (n w)"), 1e-6)

                if a == 1:
                    statistics(0)
                    normalise(0)
                    prepare(0)
                    statistics(1)
                else:
                    dve.wait_ge(sm("k0_scr"), 16)
                    prepare(0)
                for at, step in enumerate(PLAN[a]):
                    if step[0] == "M":
                        _, u, (st, t0, w, i0, nh) = step
                        dve.wait_ge(sm(f"mxp{a}"), m + 1)
                        dve.tensor_reduce(MX[:, u % 2, t0 // CH, st, i0:i0 + nh],
                                          bank(m % 4)[:, 0:nh * w].rearrange("p (i t) -> p i t", i=nh), AX, ALU.max)\
                            .then_inc(sm(f"mxfree{a}"), 1)
                        m += 1
                        if step[2] != max_items(units[u], a)[-1]:
                            continue
                        dve.wait_ge(sm(f"mxfree{a}"), m)
                        if u >= 2:
                            dve.wait_ge(sm(f"mxfree{a}"), shift_item(a, u - 2) + 1)
                        top = MX[:, u % 2, 0]
                        if a == 1 and units[u][1] == 1:
                            link(dve.tensor_tensor(top, top, MX[:, u % 2, 1], ALU.max))
                        link(dve.tensor_scalar(MP[:, u % 2, :, 0:4], top, -1.0, None, ALU.mult))
                        link(dve.scalar_tensor_tensor(out=MR[:, :, :], in0=top, scalar=-1.0, in1=MP[:, u % 2, :, 0:4],
                                                      op0=ALU.mult, op1=ALU.subtract))
                        link(dve.tensor_copy(MP[:, u % 2, :, 4:8], MR[:, :, :]))
                        dve.tensor_tensor(MP[:, u % 2, :, 8:12], MR[:, :, :], MP[:, u % 2, :, 4:8], ALU.subtract)\
                            .then_inc(sm(f"mp{a}"), 1)
                        dve.wait_ge(sm(f"mp{a}"), u + 1)
                    elif step[0] == "T":
                        u = step[1]
                        dve.wait_ge(sm(f"mxp{a}"), m + 1)
                        if u >= 2:
                            dve.wait_ge(sm(f"mrow{a}_{u % 2}"), 16 * (u // 2))
                        dve.tensor_copy(MT[:, u % 2, :], bank(m % 4)[0:12, 0:CH // 2].bitcast(BF16))\
                            .then_inc(sm(f"mxfree{a}"), 1)
                        m += 1
                    elif step[0] == "N":
                        normalise(step[1], (step[2],))
                    elif step[0] == "Q" and a == 1:
                        scaled = scale(step[1])
                        piece = 0
                    elif step[0] == "R":
                        piece = split_piece(step[1], step[2], scaled, piece)
                    elif step[0] == "Y":
                        settle()
                        add_back(k, 1.0, 0, NCH // 2)
                    elif step[0] == "F":
                        _, b, c, i = step
                        c = 2 * b + c
                        piece0 = c * CH + i * CH // FP
                        cols = slice(piece0, piece0 + CH // FP)
                        if i == 0:
                            if a == 0 and c == NCH - 1:
                                dve.wait_ge(sm("x_attn0"), NCH - 1)
                                for q in range(NCH - 1):
                                    moments(q)
                                normalise_tiles(2, 0, J)
                            for par in range(2):
                                dve.wait_ge(sm(f"ogout{a}_{par}"), 64 * 2 * (c + 1))
                        if a == 0 and c < NCH - 1:
                            dve.reciprocal(DEN[:, cols], DEN[:, cols]).then_inc(sm("rden0"), 1)
                            continue
                        link(dve.reciprocal(DEN[:, cols], DEN[:, cols]))
                        if a == 1:
                            dve.tensor_tensor(NUM[:, cols], NUM[:, cols], DEN[:, cols], ALU.mult).then_inc(sm("ctx"), 1)
                            continue
                        link(dve.tensor_tensor(NUM[:, cols], NUM[:, cols], DEN[:, cols], ALU.mult))
                        tile = X[:, c * CH // P + i, :]
                        link(dve.tensor_tensor(tile, tile, NUM[:, cols], ALU.add))
                        if i == FP - 1:
                            moments(NCH - 1)
                            normalise_tiles(2, J, NT)
                settle()
                if a == 1:
                    add_back(k, 1.0, NCH // 2, NCH)

            def keys_values():
                dve.wait_ge(sm("kf"), 1)
                link(dve.tensor_scalar(KF, KF, float(DH) ** -0.5, None, ALU.mult))
                split(KF, PARTS[0], "k0_parts")
                dve.wait_ge(sm("k0_parts"), 1)
                dve.wait_ge(sm("consts"), N_CONST)
                dve.wait_ge(sm("vp"), 1)
                dve.tensor_tensor(VF.rearrange("p (t d) -> p t d", d=D), bank(4).rearrange("p (t d) -> p t d", d=D),
                                  bvr[:, :].unsqueeze(1).to_broadcast([P, 4, D]), ALU.add).then_inc(sm("vf"), 1)
                dve.wait_ge(sm("vf"), 1)
                for t in range(TK // P):
                    mark(dve.tensor_scalar(values_of(t), VF[:, t * D:(t + 1) * D].rearrange("p (h d) -> p h d", h=NH), 0.0,
                                           None, ALU.max))
                settle()

            ffn0(0)
            attention(0, 1)
            ffn0(2)
            ffn1(3)
            attention(1, 4)
            ffn1(5)


_INS = ['L0_attn_queries', 'L0_attn_keys', 'L0_attn_values', 'L0_attn_Wq_w', 'L0_attn_Wq_b', 'L0_attn_Wk_w', 'L0_attn_Wk_b',
        'L0_attn_Wv_w', 'L0_attn_Wv_b', 'L0_ffn_w_gate_w', 'L0_ffn_w_gate_b', 'L0_ffn_W1', 'L0_ffn_b1', 'L0_ffn_W2',
        'L0_ffn_b2', 'L1_attn_W_qkv', 'L1_attn_q_scale', 'L1_attn_k_scale', 'L1_attn_W_out', 'L1_ffn_We', 'L1_ffn_be',
        'L1_ffn_Wg', 'L1_ffn_bg']


def kernel(**inputs):
    import numpy as _np
    import concourse.bacc as _bacc
    from concourse import mybir as _mybir
    from concourse.bass_utils import run_bass_kernel_spmd as _run

    nc = _bacc.Bacc("TRN2", target_bir_lowering=False, num_devices=1)
    arrays, args = {}, {}
    for name in _INS:
        a = _np.ascontiguousarray(inputs[name])
        arrays[f"in_{name}"] = a
        args[name] = nc.dram_tensor(f"in_{name}", a.shape, _mybir.dt.from_np(a.dtype), kind="ExternalInput").ap()
    out = nc.dram_tensor("out_x", (B, S, D), _mybir.dt.float32, kind="ExternalOutput").ap()
    macaron_kernel(nc, args, out)
    r = _run(nc, [arrays], core_ids=[0])
    return r.results[0]["out_x"]
```
